# Optimizing a Trainium2 kernel written in Bass

```python
import numpy as np
import jax
import jax.numpy as jnp

def _softmax(x, axis=-1):
    return jax.nn.softmax(x, axis=axis)

def _gelu(x):
    return jax.nn.gelu(x, approximate=True)

def _silu(x):
    return jax.nn.silu(x)

def _sigmoid(x):
    return jax.nn.sigmoid(x)

def _layernorm(x, axis=-1, eps=1e-05):
    m = jnp.mean(x, axis=axis, keepdims=True)
    v = jnp.var(x, axis=axis, keepdims=True)
    return (x - m) / jnp.sqrt(v + eps)

def _scatter_add(tgt, idx, src, axis=0):
    return tgt.at[idx].add(src)

def _segment_sum(src, seg, n):
    return jax.ops.segment_sum(src, seg, n)
kernel_name = 'mk_prb_d1_jaxref_r8_a51bbe'

def setup_inputs(seed: int=0):
    np.random.seed(seed)
    _w = jnp.asarray

    def _L0_attn_setup():
        import jax, jax.numpy as jnp
        import numpy as np
        L, H, D_MODEL, FFN = (2, 8, 128, 512)
        HD = D_MODEL // H
        SCALE_BASE = 64
        EPS = 1e-05

        def _layernorm(x, w, b):
            mu = x.mean(-1, keepdims=True)
            var = ((x - mu) ** 2).mean(-1, keepdims=True)
            return (x - mu) * jax.lax.rsqrt(var + EPS) * w + b

        def _groupnorm(y, w, b):
            B, S, _ = y.shape
            yg = y.reshape(B, S, H, HD)
            mu = yg.mean(-1, keepdims=True)
            var = ((yg - mu) ** 2).mean(-1, keepdims=True)
            yn = ((yg - mu) * jax.lax.rsqrt(var + EPS)).reshape(B, S, H * HD)
            return yn * w + b

        def _xpos_tables(S):
            scale_vec = (np.arange(0, HD, 2) + 0.4 * HD) / (1.4 * HD)
            power = (np.arange(S, dtype=np.float64) / SCALE_BASE)[:, None]
            scale = scale_vec[None, :] ** power
            half = HD // 2
            inv_freq = 1.0 / 10000.0 ** (np.arange(half, dtype=np.float64) / half)
            ang = np.arange(S, dtype=np.float64)[:, None] * inv_freq[None, :]
            sin, cos = (np.sin(ang), np.cos(ang))
            dup = lambda m: jnp.asarray(np.repeat(m, 2, axis=-1).astype(np.float32))
            return (dup(sin * scale), dup(cos * scale), dup(sin / scale), dup(cos / scale))

        def _rotate_every_two(x):
            x1, x2 = (x[..., ::2], x[..., 1::2])
            return jnp.stack((-x2, x1), axis=-1).reshape(x.shape)

        def _decay_mask(S):
            gammas = 1.0 - np.exp(np.linspace(np.log(1.0 / 32), np.log(1.0 / 64), H))
            n = np.arange(S)[:, None]
            m = np.arange(S)[None, :]
            diff = (n - m).astype(np.float64)
            D = np.where(n >= m, gammas[:, None, None] ** diff[None], 0.0)
            return jnp.asarray(D.astype(np.float32))
        key = jax.random.key(seed)
        ks = jax.random.split(key, 8)
        B, S = (2, 256)
        rn = lambda k, shape, s: jax.random.normal(k, shape, dtype=jnp.float32) * s
        return {'X': rn(ks[0], (B, S, D_MODEL), 1.0), 'ln1_w': jnp.ones((L, D_MODEL), jnp.float32), 'ln1_b': jnp.zeros((L, D_MODEL), jnp.float32), 'ln2_w': jnp.ones((L, D_MODEL), jnp.float32), 'ln2_b': jnp.zeros((L, D_MODEL), jnp.float32), 'WQ': rn(ks[1], (L, H, D_MODEL, HD), 1.0 / D_MODEL), 'WK': rn(ks[2], (L, H, D_MODEL, HD), 1.0 / D_MODEL), 'WV': rn(ks[3], (L, H, D_MODEL, HD), 1.0 / D_MODEL), 'gn_w': jnp.ones((L, D_MODEL), jnp.float32), 'gn_b': jnp.zeros((L, D_MODEL), jnp.float32), 'WG': rn(ks[4], (L, D_MODEL, D_MODEL), 1.0 / D_MODEL), 'WO': rn(ks[5], (L, D_MODEL, D_MODEL), 1.0 / D_MODEL), 'ffn_w1': rn(ks[6], (L, D_MODEL, FFN), 1.0 / np.sqrt(D_MODEL)), 'ffn_b1': jnp.zeros((L, FFN), jnp.float32), 'ffn_w2': rn(ks[7], (L, FFN, D_MODEL), 1.0 / np.sqrt(FFN)), 'ffn_b2': jnp.zeros((L, D_MODEL), jnp.float32)}
    _L0_attn_in = _L0_attn_setup()

    def _L0_ffn_setup():
        import jax, jax.numpy as jnp
        import numpy as np
        DIM = 128
        HIDDEN = 384
        SCALE = 1.0 / 127.0

        def _dequant(w_int, dtype):
            return w_int.astype(dtype) * jnp.asarray(SCALE, dtype)
        key = jax.random.key(seed)
        k_x, k_g, k_u, k_d = jax.random.split(key, 4)
        x = jax.random.normal(k_x, (4, 256, DIM), dtype=jnp.float32)
        w_gate = jax.random.randint(k_g, (HIDDEN, DIM), -127, 128, dtype=jnp.int32)
        w_up = jax.random.randint(k_u, (HIDDEN, DIM), -127, 128, dtype=jnp.int32)
        w_down = jax.random.randint(k_d, (DIM, HIDDEN), -127, 128, dtype=jnp.int32)
        return {'x': x, 'w_gate': w_gate, 'w_up': w_up, 'w_down': w_down}
    _L0_ffn_in = _L0_ffn_setup()
    _d = {'L0_attn_X': _L0_attn_in['X'], 'L0_attn_ln1_w': _L0_attn_in['ln1_w'], 'L0_attn_ln1_b': _L0_attn_in['ln1_b'], 'L0_attn_ln2_w': _L0_attn_in['ln2_w'], 'L0_attn_ln2_b': _L0_attn_in['ln2_b'], 'L0_attn_WQ': _L0_attn_in['WQ'], 'L0_attn_WK': _L0_attn_in['WK'], 'L0_attn_WV': _L0_attn_in['WV'], 'L0_attn_gn_w': _L0_attn_in['gn_w'], 'L0_attn_gn_b': _L0_attn_in['gn_b'], 'L0_attn_WG': _L0_attn_in['WG'], 'L0_attn_WO': _L0_attn_in['WO'], 'L0_attn_ffn_w1': _L0_attn_in['ffn_w1'], 'L0_attn_ffn_b1': _L0_attn_in['ffn_b1'], 'L0_attn_ffn_w2': _L0_attn_in['ffn_w2'], 'L0_attn_ffn_b2': _L0_attn_in['ffn_b2'], 'L0_ffn_w_gate': _L0_ffn_in['w_gate'], 'L0_ffn_w_up': _L0_ffn_in['w_up'], 'L0_ffn_w_down': _L0_ffn_in['w_down']}
    _x0 = _d['L0_attn_X']
    _d['L0_attn_X'] = jax.random.normal(jax.random.fold_in(jax.random.key(seed), 1), (8, 256, 128), dtype=_x0.dtype)
    del _x0
    return _d

def reference(L0_attn_X, L0_attn_ln1_w, L0_attn_ln1_b, L0_attn_ln2_w, L0_attn_ln2_b, L0_attn_WQ, L0_attn_WK, L0_attn_WV, L0_attn_gn_w, L0_attn_gn_b, L0_attn_WG, L0_attn_WO, L0_attn_ffn_w1, L0_attn_ffn_b1, L0_attn_ffn_w2, L0_attn_ffn_b2, L0_ffn_w_gate, L0_ffn_w_up, L0_ffn_w_down):

    def _L0_attn_ref(X, ln1_w, ln1_b, ln2_w, ln2_b, WQ, WK, WV, gn_w, gn_b, WG, WO, ffn_w1, ffn_b1, ffn_w2, ffn_b2):
        import jax, jax.numpy as jnp
        import numpy as np
        L, H, D_MODEL, FFN = (2, 8, 128, 512)
        HD = D_MODEL // H
        SCALE_BASE = 64
        EPS = 1e-05

        def _layernorm(x, w, b):
            mu = x.mean(-1, keepdims=True)
            var = ((x - mu) ** 2).mean(-1, keepdims=True)
            return (x - mu) * jax.lax.rsqrt(var + EPS) * w + b

        def _groupnorm(y, w, b):
            B, S, _ = y.shape
            yg = y.reshape(B, S, H, HD)
            mu = yg.mean(-1, keepdims=True)
            var = ((yg - mu) ** 2).mean(-1, keepdims=True)
            yn = ((yg - mu) * jax.lax.rsqrt(var + EPS)).reshape(B, S, H * HD)
            return yn * w + b

        def _xpos_tables(S):
            scale_vec = (np.arange(0, HD, 2) + 0.4 * HD) / (1.4 * HD)
            power = (np.arange(S, dtype=np.float64) / SCALE_BASE)[:, None]
            scale = scale_vec[None, :] ** power
            half = HD // 2
            inv_freq = 1.0 / 10000.0 ** (np.arange(half, dtype=np.float64) / half)
            ang = np.arange(S, dtype=np.float64)[:, None] * inv_freq[None, :]
            sin, cos = (np.sin(ang), np.cos(ang))
            dup = lambda m: jnp.asarray(np.repeat(m, 2, axis=-1).astype(np.float32))
            return (dup(sin * scale), dup(cos * scale), dup(sin / scale), dup(cos / scale))

        def _rotate_every_two(x):
            x1, x2 = (x[..., ::2], x[..., 1::2])
            return jnp.stack((-x2, x1), axis=-1).reshape(x.shape)

        def _decay_mask(S):
            gammas = 1.0 - np.exp(np.linspace(np.log(1.0 / 32), np.log(1.0 / 64), H))
            n = np.arange(S)[:, None]
            m = np.arange(S)[None, :]
            diff = (n - m).astype(np.float64)
            D = np.where(n >= m, gammas[:, None, None] ** diff[None], 0.0)
            return jnp.asarray(D.astype(np.float32))
        B, S, _ = X.shape
        sinq, cosq, sink, cosk = _xpos_tables(S)
        Dm = _decay_mask(S)
        for i in range(L):
            Xn = _layernorm(X, ln1_w[i], ln1_b[i])
            Q = jnp.einsum('bsd,hdk->bhsk', Xn, WQ[i])
            K = jnp.einsum('bsd,hdk->bhsk', Xn, WK[i])
            V = jnp.einsum('bsd,hdk->bhsk', Xn, WV[i])
            Q = Q * cosq + _rotate_every_two(Q) * sinq
            K = K * cosk + _rotate_every_two(K) * sink
            scores = jnp.einsum('bhsk,bhtk->bhst', Q, K) * Dm[None]
            Yh = jnp.einsum('bhst,bhtk->bhsk', scores, V)
            Y = Yh.transpose(0, 2, 1, 3).reshape(B, S, H * HD)
            Y = _groupnorm(Y, gn_w[i], gn_b[i])
            G = jax.nn.silu(Xn @ WG[i])
            Y = G * Y @ WO[i] + X
            Yn = _layernorm(Y, ln2_w[i], ln2_b[i])
            X = jax.nn.silu(Yn @ ffn_w1[i] + ffn_b1[i]) @ ffn_w2[i] + ffn_b2[i] + Y
        return X

    def _L0_ffn_ref(x, w_gate, w_up, w_down):
        import jax, jax.numpy as jnp
        import numpy as np
        DIM = 128
        HIDDEN = 384
        SCALE = 1.0 / 127.0

        def _dequant(w_int, dtype):
            return w_int.astype(dtype) * jnp.asarray(SCALE, dtype)
        wg = _dequant(w_gate, x.dtype)
        wu = _dequant(w_up, x.dtype)
        wd = _dequant(w_down, x.dtype)
        gate = jnp.einsum('bsd,hd->bsh', x, wg)
        up = jnp.einsum('bsd,hd->bsh', x, wu)
        h = jax.nn.silu(gate) * up
        return jnp.einsum('bsh,dh->bsd', h, wd)
    x = L0_attn_X
    xn = _layernorm(x, axis=-1)
    x = x + _L0_attn_ref(xn, L0_attn_ln1_w, L0_attn_ln1_b, L0_attn_ln2_w, L0_attn_ln2_b, L0_attn_WQ, L0_attn_WK, L0_attn_WV, L0_attn_gn_w, L0_attn_gn_b, L0_attn_WG, L0_attn_WO, L0_attn_ffn_w1, L0_attn_ffn_b1, L0_attn_ffn_w2, L0_attn_ffn_b2) + _L0_ffn_ref(xn, L0_ffn_w_gate, L0_ffn_w_up, L0_ffn_w_down)
    return x

_drawn_inputs = setup_inputs


def setup_inputs(seed=0):
    import zlib

    import numpy as np

    out = dict(_drawn_inputs(seed))
    spreads = {'L0_attn_ln1_w': (1.0, 0.6),
     'L0_attn_ln1_b': (0.0, 0.8),
     'L0_attn_ln2_w': (1.0, 0.6),
     'L0_attn_ln2_b': (0.0, 0.8),
     'L0_attn_gn_w': (1.0, 0.6),
     'L0_attn_gn_b': (0.0, 0.8),
     'L0_attn_ffn_b1': (0.0, 2.0),
     'L0_attn_ffn_b2': (0.0, 2.0)}
    factors = {'L0_attn_WQ': 8.0,
     'L0_attn_WK': 8.0,
     'L0_attn_WV': 8.0,
     'L0_attn_WG': 8.0,
     'L0_attn_WO': 8.0,
     'L0_attn_ffn_w1': 8.0,
     'L0_attn_ffn_w2': 8.0}
    for name, (base, spread) in spreads.items():
        noise = np.random.default_rng([zlib.crc32(name.encode()), seed]).standard_normal(out[name].shape)
        drawn = base * np.exp(spread * noise) if base else spread * noise
        out[name] = jnp.asarray(drawn.astype(out[name].dtype))
    for name, factor in factors.items():
        out[name] = (out[name] * factor).astype(out[name].dtype)
    return out
```

```python
from contextlib import ExitStack

import numpy as np

import concourse.bass as bass
from concourse import mybir

F32 = mybir.dt.float32
I32 = mybir.dt.int32
ALU = mybir.AluOpType
ACT = mybir.ActivationFunctionType
AX_X = mybir.AxisListType.X

P = 128
B, S, D = 8, 256, 128
L, H = 2, 8
HD = D // H
FFN = 512
HID = 384
T = S // P
G = 4
NF = FFN // P
NS = HID // P
EPS = 1e-5
QSCALE = float(np.float32(1.0 / 127.0))
LAST_LAG = 3
N_ITER = B + LAST_LAG
LOOP_START = LAST_LAG + 1
LN1W, LN1B, LN2W, LN2B, GNB, B1 = 0, L, 2 * L, 3 * L, 4 * L, 5 * L
NVEC = 5 * L + L * NF


def constants():
    half = HD // 2
    pos = np.arange(S, dtype=np.float64)
    scale = ((np.arange(0, HD, 2) + 0.4 * HD) / (1.4 * HD))[None, :] ** (pos / 64)[:, None]
    ang = pos[:, None] * (1.0 / 10000.0 ** (np.arange(half, dtype=np.float64) / half))[None, :]
    gamma = 1.0 - np.exp(np.linspace(np.log(1.0 / 32), np.log(1.0 / 64), H))
    sign = np.tile([-1.0, 1.0], half)
    cos, sin = np.empty((S, 2, H, HD)), np.empty((S, 2, H, HD))
    for part, (sc, g) in enumerate(((scale, 1.0), (1.0 / scale, -1.0))):
        decay = gamma[None, :] ** (g * pos[:, None])
        cos[:, part] = np.repeat(np.cos(ang) * sc, 2, -1)[:, None, :] * decay[:, :, None]
        sin[:, part] = (np.repeat(np.sin(ang) * sc, 2, -1) * sign)[:, None, :] * decay[:, :, None]
    tile = lambda a: a.reshape(T, P, 2 * D).transpose(1, 0, 2).reshape(P, T * 2 * D)
    f = np.arange(P)
    rotation = np.concatenate([tile(cos), tile(sin)], 1).astype(np.float32)
    masks = np.concatenate([
        np.eye(P),
        f[None, :] >= f[:, None],
        f[None, :] // HD == f[:, None] // HD,
        (np.arange(H)[None, :] == f[:, None] // HD) / HD,
        ((f // HD) % 2 == 0)[:, None], ((f // HD) % 2 == 1)[:, None],
    ], 1).astype(np.float32)
    spread = (np.arange(T * H)[:, None, None] == (np.arange(T)[:, None] * H + f[None, :] // HD)[None]).astype(np.float32)
    return {"rotation": rotation, "masks": masks, "spread": spread.reshape(T * H, T * D)}


IDENT, CAUSAL, SAMEHEAD, HEADMEAN, EVENODD = 0, P, 2 * P, 3 * P, 3 * P + H
NMASK = 3 * P + H + 2


def retention_kernel(nc, x, ln1_w, ln1_b, ln2_w, ln2_b, WQ, WK, WV, gn_w, gn_b, WG, WO,
                     ffn_w1, ffn_b1, ffn_w2, ffn_b2, w_gate, w_up, w_down,
                     rotation, masks, spread, out):
    ctx = ExitStack()
    with ctx:
        def sb(name, shape, dt=F32):
            return ctx.enter_context(nc.sbuf_tensor(name, shape, dt))

        def sem(name):
            return ctx.enter_context(nc.semaphore(name))

        def sem2(name):
            return [sem(f"{name}{s}") for s in range(L)]

        xall = sb("xall", [P, B * T, D])
        rot = sb("rot", [P, 2, T, 2 * D])
        msk = sb("msk", [P, NMASK])
        spr = sb("spr", [T * H, T, D])
        wqkv = [sb(f"wqkv{s}", [P, 3, H, HD]) for s in range(L)]
        wg = [sb(f"wg{s}", [P, D]) for s in range(L)]
        wo = [sb(f"wo{s}", [P, D]) for s in range(L)]
        w1 = [sb(f"w1_{s}", [P, FFN]) for s in range(L)]
        w2 = [sb(f"w2_{s}", [P, NF, D]) for s in range(L)]
        b2 = [sb(f"b2_{s}", [P, D]) for s in range(L)]
        gw = [sb(f"gw{s}", [T * H, D]) for s in range(L)]
        gspread = [sb(f"gspread{s}", [T * H, T, D]) for s in range(L)]
        vrow = sb("vrow", [NVEC, P])
        vcol = sb("vcol", [P, NVEC])
        vmean = [sb(f"vmean{s}", [P, H]) for s in range(L)]
        half = sb("half", [P, T * H])
        eps = sb("eps", [P, T])
        qint = [sb(f"qint{k}", [P, NS, P], I32) for k in range(3)]
        qflt = [sb(f"qflt{k}", [P, NS, P]) for k in range(3)]
        sw = [sb(f"sw{k}", [P, NS, P]) for k in range(3)]
        xn = sb("xn", [P, T, D])
        x1 = sb("x1", [P, T, D])
        lin = [xn, x1]
        resid = [sb(f"resid{s}", [P, T, D]) for s in range(L)]
        nst = L * 2 + 1
        st = [sb(f"st{k}", [P, T, 6]) for k in range(nst)]
        mv = [sb(f"mv{k}", [P, T, 2]) for k in range(nst)]
        ve = [sb(f"ve{k}", [P, T]) for k in range(nst)]
        rs = [sb(f"rs{k}", [P, T]) for k in range(nst)]
        nrm = [sb(f"nrm{s}", [P, T, D]) for s in range(L)]
        xT = [sb(f"xT{s}", [P, S]) for s in range(L)]
        rcos = [sb(f"rcos{s}", [P, T, 2 * D]) for s in range(L)]
        rsin = [sb(f"rsin{s}", [P, T, 2 * D]) for s in range(L)]
        qk = [sb(f"qk{s}", [P, T, 2 * D]) for s in range(L)]
        vpad = [sb(f"vpad{s}", [P, T, G, 4, HD]) for s in range(L)]
        gT = [sb(f"gT{s}", [P, S]) for s in range(L)]
        qT = [sb(f"qT{s}", [P, S]) for s in range(L)]
        kT = [sb(f"kT{s}", [P, 2, S]) for s in range(L)]
        stm = [sb(f"stm{s}", [P, D]) for s in range(L)]
        sc = [sb(f"sc{s}", [P, G, 2 * T, P]) for s in range(L)]
        yT = [sb(f"yT{s}", [P, S]) for s in range(L)]
        ysq = [sb(f"ysq{s}", [P, S]) for s in range(L)]
        gve = [sb(f"gve{s}", [P, T * H]) for s in range(L)]
        grs = [sb(f"grs{s}", [P, T * H]) for s in range(L)]
        grT = [sb(f"grT{s}", [T * H, P]) for s in range(L)]
        ys = [sb(f"ys{s}", [P, S]) for s in range(L)]
        zT = [sb(f"zT{s}", [P, S]) for s in range(L)]
        yres = [sb(f"yres{s}", [P, T, D]) for s in range(L)]
        yb = [sb(f"yb{s}", [P, T, D]) for s in range(L)]
        ybx = sb("ybx", [P, T, D])
        nrm2 = [sb(f"nrm2_{s}", [P, T, D]) for s in range(L)]
        y2T = [sb(f"y2T{s}", [P, S]) for s in range(L)]
        hT = [sb(f"hT{s}", [P, NF, S]) for s in range(L)]
        snT = sb("snT", [P, S])
        sg = sb("sg", [P, NS, S])
        sh = sb("sh", [P, NS, S])
        osb = sb("osb", [P, T, D])

        SC = ctx.enter_context(nc.psum_tensor("SC", [P, G, 512], F32))
        A = [ctx.enter_context(nc.psum_tensor(f"A{s}", [P, 512], F32)) for s in range(L)]
        F = [ctx.enter_context(nc.psum_tensor(f"F{k}", [P, 512], F32)) for k in range(2)]

        ld_x, ld_msk, ld_vec, ld_rot, ld_spr, ld_q = (sem(n) for n in ("ld_x", "ld_msk", "ld_vec", "ld_rot", "ld_spr", "ld_q"))
        ld_qkv, ld_wg, ld_wo, ld_w1, ld_w2, ld_b2, ld_gw = (
            sem2(n) for n in ("ld_qkv", "ld_wg", "ld_wo", "ld_w1", "ld_w2", "ld_b2", "ld_gw"))
        vec_turned, vec_ready, half_ready, pad_ready, qflt_ready, sw_turned, sw_ready = (
            sem(n) for n in ("vec_turned", "vec_ready", "half_ready", "pad_ready", "qflt_ready", "sw_turned", "sw_ready"))
        wv_sum, wv_mean, wv_ready, gspread_ready = (
            sem2(n) for n in ("wv_sum", "wv_mean", "wv_ready", "gspread_ready"))
        ln_stats, ln_mv, ln_eps, ln_rstd, ln_done = (
            [sem(f"{n}{k}") for k in range(nst)] for n in ("ln_stats", "ln_mv", "ln_eps", "ln_rstd", "ln_done"))
        x_turned, xT_ready, qkv_done, g_done, rot_parts, qk_ready, v_ready, g_ready = (
            sem2(n) for n in ("x_turned", "xT_ready", "qkv_done", "g_done", "rot_parts", "qk_ready", "v_ready", "g_ready"))
        qk_turned, qkT_ready, state_done, scores_done, state_ready, scores_ready, y_done, yT_ready, ysq_ready = (
            sem2(n) for n in ("qk_turned", "qkT_ready", "state_done", "scores_done", "state_ready", "scores_ready",
                              "y_done", "yT_ready", "ysq_ready"))
        gvar_done, gvar_ready, grstd_ready, grstd_turned, grstdT_ready, grstd_spread, ys_ready, z_ready, o_done, yres_ready = (
            sem2(n) for n in ("gvar_done", "gvar_ready", "grstd_ready", "grstd_turned", "grstdT_ready", "grstd_spread",
                              "ys_ready", "z_ready", "o_done", "yres_ready"))
        resid_ready = sem2("resid_ready")
        yb_ready, y_turned, y2T_ready, ffn2_done, x1_ready = (
            sem2(n) for n in ("yb_ready", "y_turned", "y2T_ready", "ffn2_done", "ffn_out"))
        ffn1_done = [[sem(f"ffn1_done{s}_{k}") for k in range(2)] for s in range(L)]
        h_ready = [[sem(f"h_ready{s}_{k}") for k in range(2)] for s in range(L)]
        s_turned, snT_ready, down_done, side_ready, ybx_ready, stored = (
            sem(n) for n in ("s_turned", "snT_ready", "down_done", "side_ready", "ybx_ready", "stored"))
        gu_done = [sem(f"gu_done{k}") for k in range(NS)]
        sg_ready = [sem(f"sg_ready{k}") for k in range(NS)]
        sh_ready = [sem(f"sh_ready{k}") for k in range(NS)]

        def on(j):
            return not isinstance(j, int) or 0 <= j < B

        def wait(eng, s, value):
            if isinstance(value, int):
                if value > 0:
                    eng.wait_ge(s, value)
            else:
                eng.wait_ge(s, value)

        def passed(eng, s, j):
            wait(eng, s, j + 1)

        def bank_free(eng, *users):
            for s, j in users:
                if on(j):
                    passed(eng, s, j)
                    return

        def run(eng, iteration):
            for i in range(LOOP_START):
                iteration(i)
            with eng.Fori(LOOP_START, B - 1) as i:
                iteration(i)
            for i in range(B - 1, N_ITER):
                iteration(i)

        col = lambda k: vcol[:, k:k + 1]
        ident = msk[:, IDENT:IDENT + P]

        vp_flat = [vpad[s][:, :, :, :, :].rearrange("p t g a k -> p t g (a k)") for s in range(L)]

        def v_heads(s, t):
            v = vpad[s][:, t, :, :, :]
            return v[:, :, 0::3, :]

        SIDE_BANK = [1, 0, 0]

        block = ctx.enter_context(nc.Block())

        @block.sync
        def _(sp):
            x_v = x.rearrange("b (t p) d -> p (b t) d", p=P)
            sp.dma_start(xall[:, 0:T, :], x_v[:, 0:T, :]).then_inc(ld_x, 16)
            sp.dma_start(msk[:, :], masks).then_inc(ld_msk, 16)
            for k, (v, n) in enumerate(((ln1_w, L), (ln1_b, L), (ln2_w, L), (ln2_b, L), (gn_b, L))):
                sp.dma_start(vrow[k * L:(k + 1) * L, :], v).then_inc(ld_vec, 16)
            sp.dma_start(vrow[B1:B1 + L * NF, :], ffn_b1.rearrange("l (n p) -> (l n) p", p=P)).then_inc(ld_vec, 16)
            for k, W in enumerate((WQ, WK, WV)):
                sp.dma_start(wqkv[0][:, k, :, :], W[0].rearrange("h d k -> d h k")).then_inc(ld_qkv[0], 16)
            sp.dma_start(rot[:, :, :, :], rotation.rearrange("p (c t n) -> p c t n", c=2, t=T)).then_inc(ld_rot, 16)
            for k, W in enumerate((w_gate, w_up)):
                sp.dma_start(qint[k][:, :, :], W.rearrange("(n p) d -> p n d", p=P)).then_inc(ld_q, 16)
            sp.dma_start(qint[2][:, :, :], w_down.rearrange("p (n q) -> p n q", n=NS)).then_inc(ld_q, 16)
            for s in range(L):
                sp.dma_start(gw[s][:, :], gn_w[s:s + 1, :].partition_broadcast(T * H)).then_inc(ld_gw[s], 16)
            for k, W in enumerate((WQ, WK, WV)):
                sp.dma_start(wqkv[1][:, k, :, :], W[1].rearrange("h d k -> d h k")).then_inc(ld_qkv[1], 16)

            o_v = out.rearrange("b (t p) d -> p (b t) d", p=P)

            def iteration(i):
                j = i - 3
                if on(j):
                    passed(sp, x1_ready[1], j)
                    sp.dma_start(o_v[:, bass.ds(j * T, T), :], osb[:, :, :]).then_inc(stored, 16)
            run(sp, iteration)
            sp.wait_ge(stored, 16 * B)

        @block.scalar
        def _(act):
            act.dma_start(wg[0][:, :], WG[0]).then_inc(ld_wg[0], 16)
            act.dma_start(wo[0][:, :], WO[0]).then_inc(ld_wo[0], 16)
            act.dma_start(xall[:, T:, :], x.rearrange("b (t p) d -> p (b t) d", p=P)[:, T:, :]).then_inc(ld_x, 16)
            act.dma_start(spr[:, :, :], spread.rearrange("p (t d) -> p t d", t=T)).then_inc(ld_spr, 16)
            for s in range(L):
                act.dma_start(w1[s][:, :], ffn_w1[s]).then_inc(ld_w1[s], 16)
                act.dma_start(w2[s][:, :, :], ffn_w2[s].rearrange("(n p) d -> p n d", p=P)).then_inc(ld_w2[s], 16)
                act.dma_start(b2[s][:, :], ffn_b2[s:s + 1, :].partition_broadcast(P)).then_inc(ld_b2[s], 16)
            act.dma_start(wg[1][:, :], WG[1]).then_inc(ld_wg[1], 16)
            act.dma_start(wo[1][:, :], WO[1]).then_inc(ld_wo[1], 16)

            def x_affine(s, j):
                passed(act, x_turned[s], j)
                wait(act, g_done[s], j)
                nc.scalar.activation(xT[s][:, :], A[s][:, 0:S], ACT.Identity, bias=col(LN1B + s),
                                     scale=col(LN1W + s)).then_inc(xT_ready[s], 1)

            def gate(s, j):
                passed(act, g_done[s], j)
                wait(act, z_ready[s], j)
                nc.scalar.activation(gT[s][:, :], A[s][:, 0:S], ACT.Silu).then_inc(g_ready[s], 1)

            def values(s, j):
                passed(act, rot_parts[s], j)
                wait(act, y_done[s], j)
                for t in range(T):
                    v = nc.scalar.activation(v_heads(s, t), SC[:, 2 * s + t, 2 * D:3 * D].rearrange(
                        "p (g a k) -> p g a k", g=G, a=2), ACT.Copy)
                v.then_inc(v_ready[s], 1)

            def qk_evacuate(s, j):
                passed(act, qk_turned[s], j)
                wait(act, y_done[s], j)
                nc.scalar.activation(qT[s][:, :], A[s][:, 0:S], ACT.Copy)
                for r in range(2):
                    k = nc.scalar.activation(kT[s][:, r, :], A[s][:, S:2 * S], ACT.Identity,
                                             scale=msk[:, EVENODD + r:EVENODD + r + 1])
                k.then_inc(qkT_ready[s], 1)

            def y_evacuate(s, j):
                passed(act, y_done[s], j)
                wait(act, ys_ready[s], j)
                nc.scalar.activation(yT[s][:, :], A[s][:, 0:S], ACT.Copy).then_inc(yT_ready[s], 1)
                wait(act, gvar_done[s], j)
                nc.scalar.activation(ysq[s][:, :], A[s][:, 0:S], ACT.Square).then_inc(ysq_ready[s], 1)

            def y_affine(s, j):
                passed(act, y_turned[s], j)
                wait(act, ffn1_done[s][1], j)
                nc.scalar.activation(y2T[s][:, :], F[s][:, 0:S], ACT.Identity, bias=col(LN2B + s),
                                     scale=col(LN2W + s)).then_inc(y2T_ready[s], 1)

            def ffn_silu(s, k, j):
                wait(act, ffn2_done[s], j)
                passed(act, ffn1_done[s][k], j)
                for r in range(2):
                    n = 2 * k + r
                    h = nc.scalar.activation(hT[s][:, n, :], F[k][:, r * S:(r + 1) * S], ACT.Silu,
                                             bias=col(B1 + s * NF + n))
                h.then_inc(h_ready[s][k], 1)

            def side_input(j):
                passed(act, s_turned, j)
                wait(act, gu_done[NS - 1], j)
                nc.scalar.activation(snT[:, :], F[1][:, 0:S], ACT.Copy).then_inc(snT_ready, 1)

            def side_silu(k, j):
                passed(act, gu_done[k], j)
                wait(act, sh_ready[k], j)
                nc.scalar.activation(sg[:, k, :], F[SIDE_BANK[k]][:, 0:S], ACT.Silu).then_inc(sg_ready[k], 1)

            def iteration(i):
                j0, j1, j2, j3 = i, i - 1, i - 2, i - 3
                if on(j0):
                    x_affine(0, j0)
                if on(j1):
                    y_affine(0, j1)
                if on(j0):
                    side_input(j0)
                    gate(0, j0)
                if on(j1):
                    ffn_silu(0, 0, j1)
                if on(j0):
                    values(0, j0)
                if on(j1):
                    ffn_silu(0, 1, j1)
                if on(j0):
                    qk_evacuate(0, j0)
                if on(j2):
                    x_affine(1, j2)
                if on(j0):
                    side_silu(0, j0)
                if on(j2):
                    gate(1, j2)
                if on(j0):
                    side_silu(1, j0)
                if on(j2):
                    values(1, j2)
                if on(j3):
                    y_affine(1, j3)
                    ffn_silu(1, 0, j3)
                if on(j2):
                    qk_evacuate(1, j2)
                if on(j3):
                    ffn_silu(1, 1, j3)
                if on(j0):
                    y_evacuate(0, j0)
                    side_silu(2, j0)
                if on(j2):
                    y_evacuate(1, j2)

            act.wait_ge(vec_ready, 1)
            act.wait_ge(pad_ready, 1)
            run(act, iteration)

        @block.gpsimd
        def _(pool):
            nc.gpsimd.memset(half[:, :], -0.5)
            nc.gpsimd.memset(eps[:, :], EPS).then_inc(half_ready, 1)
            for s in range(L):
                last = nc.gpsimd.memset(vpad[s][:, :, :, :, :], 0.0)
            last.then_inc(pad_ready, 1)
            pool.wait_ge(half_ready, 1)

            def ln_root(k, j):
                passed(pool, ln_mv[k], j)
                nc.gpsimd.tensor_tensor(ve[k][:, :], mv[k][:, :, 1], eps[:, :], ALU.add).then_inc(ln_eps[k], 1)
                passed(pool, ln_eps[k], j)
                wait(pool, ln_done[k], j)
                nc.gpsimd.tensor_tensor(rs[k][:, :], ve[k][:, :], half[:, 0:T], ALU.pow).then_inc(ln_rstd[k], 1)

            def rotate_sum(s, j):
                passed(pool, rot_parts[s], j)
                wait(pool, state_done[s], j)
                nc.gpsimd.tensor_tensor(qk[s][:, :, :], rcos[s][:, :, :], rsin[s][:, :, :], ALU.add).then_inc(qk_ready[s], 1)

            def group_root(s, j):
                passed(pool, gvar_ready[s], j)
                wait(pool, grstd_turned[s], j)
                nc.gpsimd.tensor_tensor(grs[s][:, :], gve[s][:, :], half[:, :], ALU.pow).then_inc(grstd_ready[s], 1)

            def residual_plus_bias(s, j):
                passed(pool, yres_ready[s], j)
                wait(pool, x1_ready[s], j)
                nc.gpsimd.tensor_tensor(yb[s][:, :, :], yres[s][:, :, :],
                                        b2[s][:, :].unsqueeze(1).broadcast_to([P, T, D]), ALU.add).then_inc(yb_ready[s], 1)
                if s == L - 1:
                    passed(pool, yb_ready[s], j)
                    passed(pool, side_ready, j)
                    nc.gpsimd.tensor_tensor(ybx[:, :, :], yb[s][:, :, :], xall[:, bass.ds(j * T, T), :],
                                            ALU.add).then_inc(ybx_ready, 1)

            def iteration(i):
                j0, j1, j2, j3 = i, i - 1, i - 2, i - 3
                if on(j0):
                    rotate_sum(0, j0)
                if on(j1):
                    residual_plus_bias(0, j1)
                if on(j3):
                    ln_root(4, j3)
                if on(j2):
                    rotate_sum(1, j2)
                if on(j1):
                    ln_root(2, j1)
                if on(j3):
                    residual_plus_bias(1, j3)
                if on(j0):
                    group_root(0, j0)
                if on(i + 1):
                    ln_root(0, i + 1)
                    ln_root(1, i + 1)
                if on(j2):
                    group_root(1, j2)
                if on(j0):
                    ln_root(3, j0)

            pool.wait_ge(ld_b2[0], 16)
            pool.wait_ge(ld_b2[1], 16)
            ln_root(0, 0)
            ln_root(1, 0)
            run(pool, iteration)

        @block.vector
        def _(dve):
            def ln_statistics(k, src, j):
                wait(dve, ln_eps[k], j)
                if not isinstance(j, int):
                    passed(dve, ld_x, j)
                for t in range(T):
                    b = nc.vector.bn_stats(st[k][:, t, :], src(t))
                b.then_inc(ln_stats[k], 1)
                dve.wait_ge(ld_x, 32)
                passed(dve, ln_stats[k], j)
                for t in range(T):
                    b = nc.vector.bn_aggr(mv[k][:, t, :], st[k][:, t, :])
                b.then_inc(ln_mv[k], 1)

            def ln_normalise(k, dst, src, j):
                passed(dve, ln_rstd[k], j)
                for t in range(T):
                    b = nc.vector.tensor_scalar(dst[:, t, :], src(t), mv[k][:, t, 0:1], rs[k][:, t:t + 1],
                                                ALU.subtract, ALU.mult)
                b.then_inc(ln_done[k], 1)

            def x_tile(j):
                return lambda t: xall[:, bass.ds(j * T + t, 1), :].rearrange("p a d -> p (a d)")

            def tile_of(buf):
                return lambda t: buf[:, t, :]

            def input_stats(j):
                ln_statistics(0, x_tile(j), j)

            def input_norm(j):
                if not (isinstance(j, int) and j == 0):
                    passed(dve, s_turned, j - 1)
                    passed(dve, resid_ready[0], j - 1)
                ln_normalise(0, xn, x_tile(j), j)

            def ln1_stats(s, j):
                passed(dve, [ln_done[0], x1_ready[0]][s], j)
                ln_statistics(1 + s, tile_of(lin[s]), j)

            def ln1_norm(s, j):
                wait(dve, x_turned[s], j)
                ln_normalise(1 + s, nrm[s], tile_of(lin[s]), j)

            def keep_residual(s, j):
                passed(dve, ln_done[1 + s], j)
                wait(dve, yres_ready[s], j)
                nc.vector.tensor_copy(resid[s][:, :, :], lin[s][:, :, :]).then_inc(resid_ready[s], 1)

            def rotate(s, j):
                passed(dve, qkv_done[s], j)
                wait(dve, qk_ready[s], j)
                q = SC[:, 2 * s:2 * s + 2, 0:2 * D]
                nc.vector.tensor_tensor(rcos[s][:, :, :], q, rot[:, 0, :, :], ALU.mult)
                for t in range(T):
                    pairs = SC[:, 2 * s + t, 0:2 * D].rearrange("p (n a) -> p n a", a=2)[:, :, ::-1]
                    r = nc.vector.tensor_tensor(rsin[s][:, t, :].rearrange("p (n a) -> p n a", a=2), pairs,
                                                rot[:, 1, t, :].rearrange("p (n a) -> p n a", a=2), ALU.mult)
                r.then_inc(rot_parts[s], 1)

            def mask_state(s, j):
                passed(dve, state_done[s], j)
                wait(dve, y_done[s], j)
                nc.vector.tensor_tensor(stm[s][:, :], A[s][:, 0:D], msk[:, SAMEHEAD:SAMEHEAD + P],
                                        ALU.mult).then_inc(state_ready[s], 1)

            def mask_scores(s, j):
                passed(dve, scores_done[s], j)
                causal = msk[:, CAUSAL:CAUSAL + P].unsqueeze(1).broadcast_to([P, 2 * T, P])
                for g in range(G):
                    m = nc.vector.tensor_tensor(sc[s][:, g, :, :], SC[:, g, :].rearrange("p (a n) -> p a n", n=P),
                                                causal, ALU.mult)
                m.then_inc(scores_ready[s], 1)

            def group_variance(s, j):
                passed(dve, gvar_done[s], j)
                wait(dve, grstd_ready[s], j)
                nc.vector.tensor_scalar(gve[s][:, :], A[s][:, 0:T * H], EPS, None, ALU.add).then_inc(gvar_ready[s], 1)

            def group_rstd(s, j):
                passed(dve, grstd_turned[s], j)
                wait(dve, grstd_spread[s], j)
                nc.vector.tensor_copy(grT[s][:, :], A[s][0:T * H, 0:P]).then_inc(grstdT_ready[s], 1)

            def gate_y(s, j):
                passed(dve, grstd_spread[s], j)
                passed(dve, yT_ready[s], j)
                nc.vector.tensor_tensor(ys[s][:, :], A[s][:, 0:S], yT[s][:, :], ALU.mult).then_inc(ys_ready[s], 1)
                passed(dve, ys_ready[s], j)
                passed(dve, g_ready[s], j)
                wait(dve, o_done[s], j)
                nc.vector.scalar_tensor_tensor(out=zT[s][:, :], in0=ys[s][:, :], scalar=col(GNB + s), in1=gT[s][:, :],
                                               op0=ALU.add, op1=ALU.mult).then_inc(z_ready[s], 1)

            def add_residual(s, j):
                passed(dve, o_done[s], j)
                passed(dve, resid_ready[s], j)
                wait(dve, yb_ready[s], j)
                nc.vector.tensor_tensor(yres[s][:, :, :], A[s][:, 0:S].rearrange("p (t d) -> p t d", t=T),
                                        resid[s][:, :, :], ALU.add).then_inc(yres_ready[s], 1)

            def ln2_stats(s, j):
                passed(dve, yres_ready[s], j)
                ln_statistics(3 + s, tile_of(yres[s]), j)

            def ln2_norm(s, j):
                wait(dve, y_turned[s], j)
                ln_normalise(3 + s, nrm2[s], tile_of(yres[s]), j)

            def layer0_out(j):
                passed(dve, ffn2_done[0], j)
                passed(dve, yb_ready[0], j)
                wait(dve, resid_ready[1], j)
                nc.vector.tensor_tensor(x1[:, :, :], F[0][:, 0:S].rearrange("p (t d) -> p t d", t=T),
                                        yb[0][:, :, :], ALU.add).then_inc(x1_ready[0], 1)

            def layer1_out(j):
                passed(dve, ffn2_done[1], j)
                passed(dve, ybx_ready, j)
                if on(j - 1):
                    wait(dve, stored, 16 * j)
                nc.vector.tensor_tensor(osb[:, :, :], F[0][:, 0:S].rearrange("p (t d) -> p t d", t=T),
                                        ybx[:, :, :], ALU.add).then_inc(x1_ready[1], 1)

            def side_product(k, j):
                passed(dve, sg_ready[k], j)
                wait(dve, down_done, j)
                nc.vector.tensor_tensor(sh[:, k, :], F[SIDE_BANK[k]][:, S:2 * S], sg[:, k, :], ALU.mult).then_inc(sh_ready[k], 1)

            def side_out(j):
                passed(dve, down_done, j)
                nc.vector.tensor_tensor(xall[:, bass.ds(j * T, T), :], F[1][:, 0:S].rearrange("p (t d) -> p t d", t=T),
                                        xall[:, bass.ds(j * T, T), :], ALU.add).then_inc(side_ready, 1)

            def side_weights():
                dve.wait_ge(ld_q, 48)
                for k in range(3):
                    q = nc.vector.tensor_scalar(qflt[k][:, :, :], qint[k][:, :, :], QSCALE, None, ALU.mult)
                q.then_inc(qflt_ready, 1)

            def side_weights_out():
                dve.wait_ge(sw_turned, 1)
                for k in range(2):
                    nc.vector.tensor_copy(sw[k][:, :, :], SC[:, 2 + k, 0:NS * P].rearrange("p (n q) -> p n q", n=NS))
                nc.vector.tensor_copy(sw[2][:, :, :], F[0][:, 0:NS * P].rearrange("p (n q) -> p n q", n=NS)).then_inc(sw_ready, 1)

            def centre_values(s):
                dve.wait_ge(ld_qkv[s], 48)
                nc.vector.tensor_reduce(vmean[s][:, :], wqkv[s][:, 2, :, :], AX_X, ALU.add).then_inc(wv_sum[s], 1)
                dve.wait_ge(wv_sum[s], 1)
                nc.vector.tensor_scalar(vmean[s][:, :], vmean[s][:, :], -1.0 / HD, None, ALU.mult).then_inc(wv_mean[s], 1)
                dve.wait_ge(wv_mean[s], 1)
                nc.vector.tensor_tensor(wqkv[s][:, 2, :, :], wqkv[s][:, 2, :, :],
                                        vmean[s][:, :].unsqueeze(2).broadcast_to([P, H, HD]), ALU.add).then_inc(wv_ready[s], 1)

            def spread_weights(s):
                dve.wait_ge(ld_gw[s], 16)
                nc.vector.tensor_tensor(gspread[s][:, :, :], spr[:, :, :],
                                        gw[s][:, :].unsqueeze(1).broadcast_to([T * H, T, D]), ALU.mult).then_inc(gspread_ready[s], 1)

            def iteration(i):
                j0, j1, j2, j3 = i, i - 1, i - 2, i - 3
                if on(j1):
                    ln2_norm(0, j1)
                if on(j0):
                    rotate(0, j0)
                if isinstance(i, int) and i == 0:
                    side_weights_out()
                if on(j3):
                    group_rstd(1, j3)
                if on(j0):
                    keep_residual(0, j0)
                if on(j3):
                    gate_y(1, j3)
                    add_residual(1, j3)
                    ln2_stats(1, j3)
                if on(j2):
                    keep_residual(1, j2)
                if on(j1):
                    layer0_out(j1)
                    ln1_stats(1, j1)
                if on(j3):
                    ln2_norm(1, j3)
                if on(j2):
                    rotate(1, j2)
                if on(j0):
                    side_product(0, j0)
                    side_product(1, j0)
                if on(j1):
                    ln1_norm(1, j1)
                if on(j0):
                    mask_state(0, j0)
                    mask_scores(0, j0)
                if on(i + 1):
                    input_stats(i + 1)
                if on(j2):
                    mask_state(1, j2)
                    mask_scores(1, j2)
                if on(j0):
                    group_variance(0, j0)
                    side_product(2, j0)
                    side_out(j0)
                if on(i + 1):
                    input_norm(i + 1)
                    ln1_stats(0, i + 1)
                if on(j0):
                    group_rstd(0, j0)
                if on(i + 1):
                    ln1_norm(0, i + 1)
                if on(j3):
                    layer1_out(j3)
                if on(j0):
                    gate_y(0, j0)
                if on(j2):
                    group_variance(1, j2)
                if on(j0):
                    add_residual(0, j0)
                    ln2_stats(0, j0)

            dve.wait_ge(ld_x, 32)
            input_stats(0)
            dve.wait_ge(vec_turned, 1)
            nc.vector.tensor_copy(vcol[:, :], A[0][:, 0:NVEC]).then_inc(vec_ready, 1)
            input_norm(0)
            ln1_stats(0, 0)
            ln1_norm(0, 0)
            centre_values(0)
            dve.wait_ge(ld_spr, 16)
            spread_weights(0)
            side_weights()
            spread_weights(1)
            centre_values(1)
            dve.wait_ge(ld_rot, 16)
            run(dve, iteration)

        @block.tensor
        def _(pe):
            mm = nc.tensor.matmul

            def x_turn(s, j):
                passed(pe, ln_done[1 + s], j)
                bank_free(pe, (yres_ready[s], j - 1))
                for t in range(T):
                    m = nc.tensor.transpose(A[s][:, t * P:(t + 1) * P], nrm[s][:, t, :], ident)
                m.then_inc(x_turned[s], 1)

            def project(s, j):
                passed(pe, xT_ready[s], j)
                bank_free(pe, *[[(scores_ready[1], i_of(s, j) - 3), (scores_ready[0], i_of(s, j) - 1)],
                                [(scores_ready[1], i_of(s, j) - 3), (scores_ready[0], i_of(s, j) - 1)]][s])
                for t in range(T):
                    m = mm(SC[:, 2 * s + t, 0:3 * D], xT[s][:, t * P:(t + 1) * P],
                           wqkv[s][:, :, :, :].rearrange("p c h k -> p (c h k)"), start=True, stop=True)
                m.then_inc(qkv_done[s], 1)
                mm(A[s][:, 0:S], wg[s][:, :], xT[s][:, :], start=True, stop=True).then_inc(g_done[s], 1)

            def qk_turn(s, j):
                passed(pe, qk_ready[s], j)
                passed(pe, g_ready[s], j)
                for c in range(2):
                    for t in range(T):
                        m = nc.tensor.transpose(A[s][:, (c * T + t) * P:(c * T + t + 1) * P],
                                                qk[s][:, t, c * D:(c + 1) * D], ident)
                m.then_inc(qk_turned[s], 1)

            def scores(s, j):
                passed(pe, qkT_ready[s], j)
                passed(pe, v_ready[s], j)
                for k in range(L):
                    jj = i_of(s, j) - [0, 2][k]
                    if on(jj):
                        passed(pe, rot_parts[k], jj)
                        passed(pe, v_ready[k], jj)
                bank_free(pe, *[[(scores_ready[1], i_of(s, j) - 3)], [(scores_ready[0], i_of(s, j))]][s])
                mm(A[s][:, 0:D], qk[s][:, 0, D:2 * D], v_heads(s, 0), start=True, stop=True).then_inc(state_done[s], 1)
                for r in range(2):
                    for t in range(T):
                        for g in range(G):
                            rows = slice(32 * g, 32 * g + 32)
                            m = mm(SC[:, g, (r * T + t) * P:(r * T + t + 1) * P], kT[s][rows, r, t * P:(t + 1) * P],
                                   qT[s][rows, t * P:(t + 1) * P], start=True, stop=True)
                m.then_inc(scores_done[s], 1)

            def attend(s, j):
                passed(pe, scores_ready[s], j)
                passed(pe, state_ready[s], j)
                for r in range(2):
                    for t in range(T):
                        for g in range(G):
                            head = vp_flat[s][:, t, g, 32 * r:32 * r + 32]
                            mm(A[s][32 * g:32 * g + 32, t * P:(t + 1) * P], head, sc[s][:, g, r * T + t, :],
                               start=(r == 0 and t == 0), stop=(r == 1 and t == 0), skip_group_check=True)
                mm(A[s][:, P:2 * P], stm[s][:, :], qT[s][:, P:2 * P], start=False, stop=True,
                   skip_group_check=True).then_inc(y_done[s], 1)

            def variance(s, j):
                passed(pe, ysq_ready[s], j)
                for t in range(T):
                    m = mm(A[s][:, t * H:(t + 1) * H], ysq[s][:, t * P:(t + 1) * P], msk[:, HEADMEAN:HEADMEAN + H],
                           start=True, stop=True)
                m.then_inc(gvar_done[s], 1)

            def rstd_turn(s, j):
                passed(pe, grstd_ready[s], j)
                nc.tensor.transpose(A[s][0:T * H, 0:P], grs[s][:, :], ident).then_inc(grstd_turned[s], 1)

            def rstd_spread(s, j):
                passed(pe, grstdT_ready[s], j)
                for t in range(T):
                    m = mm(A[s][:, t * P:(t + 1) * P], gspread[s][:, t, :], grT[s][:, :], start=True, stop=True)
                m.then_inc(grstd_spread[s], 1)

            def project_out(s, j):
                passed(pe, z_ready[s], j)
                for t in range(T):
                    m = mm(A[s][:, t * P:(t + 1) * P], zT[s][:, t * P:(t + 1) * P], wo[s][:, :], start=True, stop=True)
                m.then_inc(o_done[s], 1)

            def y_turn(s, j):
                passed(pe, ln_done[3 + s], j)
                for t in range(T):
                    m = nc.tensor.transpose(F[s][:, t * P:(t + 1) * P], nrm2[s][:, t, :], ident)
                m.then_inc(y_turned[s], 1)

            def ffn_in(s, k, j):
                for r in range(2):
                    n = 2 * k + r
                    m = mm(F[k][:, r * S:(r + 1) * S], w1[s][:, n * P:(n + 1) * P], y2T[s][:, :], start=True, stop=True)
                m.then_inc(ffn1_done[s][k], 1)

            def ffn_out(s, j):
                passed(pe, h_ready[s][0], j)
                passed(pe, h_ready[s][1], j)
                for t in range(T):
                    for n in range(NF):
                        m = mm(F[0][:, t * P:(t + 1) * P], hT[s][:, n, t * P:(t + 1) * P], w2[s][:, n, :],
                               start=(n == 0), stop=(n == NF - 1))
                m.then_inc(ffn2_done[s], 1)

            def side_turn(j):
                passed(pe, ln_done[0], j)
                for t in range(T):
                    m = nc.tensor.transpose(F[1][:, t * P:(t + 1) * P], xn[:, t, :], ident)
                m.then_inc(s_turned, 1)

            def side_in(k, j):
                passed(pe, snT_ready, j)
                b = F[SIDE_BANK[k]]
                mm(b[:, 0:S], sw[0][:, k, :], snT[:, :], start=True, stop=True)
                mm(b[:, S:2 * S], sw[1][:, k, :], snT[:, :], start=True, stop=True).then_inc(gu_done[k], 1)

            def side_down(j):
                for k in range(NS):
                    passed(pe, sh_ready[k], j)
                for t in range(T):
                    for k in range(NS):
                        m = mm(F[1][:, t * P:(t + 1) * P], sh[:, k, t * P:(t + 1) * P], sw[2][:, k, :],
                               start=(k == 0), stop=(k == NS - 1))
                m.then_inc(down_done, 1)

            def side_weights():
                pe.wait_ge(qflt_ready, 1)
                for k in range(3):
                    b = [SC[:, 2, :], SC[:, 3, :], F[0][:, :]][k]
                    for n in range(NS):
                        m = nc.tensor.transpose(b[:, n * P:(n + 1) * P], qflt[k][:, n, :], ident)
                m.then_inc(sw_turned, 1)
                pe.wait_ge(sw_ready, 1)

            def iteration(i):
                j0, j1, j2, j3 = i, i - 1, i - 2, i - 3
                if on(j0):
                    x_turn(0, j0)
                if on(j1):
                    bank_free(pe, (x1_ready[1], j3 - 1), (sh_ready[2], j0 - 1))
                    y_turn(0, j1)
                if on(j0):
                    bank_free(pe, (side_ready, j0 - 1))
                    side_turn(j0)
                    project(0, j0)
                if isinstance(i, int) and i == 0:
                    side_weights()
                if on(j3):
                    rstd_turn(1, j3)
                if on(j1):
                    passed(pe, y2T_ready[0], j1)
                    ffn_in(0, 0, j1)
                if on(j3):
                    rstd_spread(1, j3)
                if on(j1):
                    bank_free(pe, (snT_ready, j0), (side_ready, j0 - 1), (h_ready[1][1], j3 - 1))
                    ffn_in(0, 1, j1)
                if on(j0):
                    qk_turn(0, j0)
                if on(j3):
                    project_out(1, j3)
                if on(j1):
                    ffn_out(0, j1)
                if on(j2):
                    x_turn(1, j2)
                if on(j0):
                    bank_free(pe, (h_ready[0][1], j1), (snT_ready, j0))
                    side_in(0, j0)
                if on(j2):
                    project(1, j2)
                if on(j0):
                    bank_free(pe, (x1_ready[0], j1))
                    side_in(1, j0)
                    scores(0, j0)
                if on(j3):
                    bank_free(pe, (sh_ready[0], j0), (h_ready[0][1], j1), (h_ready[1][1], j3 - 1))
                    y_turn(1, j3)
                    bank_free(pe, (sh_ready[1], j0), (x1_ready[0], j1), (x1_ready[1], j3 - 1))
                    passed(pe, y2T_ready[1], j3)
                    ffn_in(1, 0, j3)
                if on(j2):
                    qk_turn(1, j2)
                if on(j3):
                    ffn_in(1, 1, j3)
                if on(j0):
                    attend(0, j0)
                if on(j2):
                    scores(1, j2)
                if on(j0):
                    variance(0, j0)
                    bank_free(pe, (h_ready[1][0], j3), (sh_ready[1], j0))
                    side_in(2, j0)
                    bank_free(pe, (h_ready[1][1], j3), (sh_ready[0], j0))
                    side_down(j0)
                if on(j2):
                    attend(1, j2)
                if on(j0):
                    rstd_turn(0, j0)
                if on(j3):
                    bank_free(pe, (sh_ready[2], j0), (h_ready[1][0], j3))
                    ffn_out(1, j3)
                if on(j0):
                    rstd_spread(0, j0)
                if on(j2):
                    variance(1, j2)
                if on(j0):
                    project_out(0, j0)

            def i_of(s, j):
                return j + 2 * s

            pe.wait_ge(ld_msk, 16)
            pe.wait_ge(ld_vec, 16 * 6)
            nc.tensor.transpose(A[0][:, 0:NVEC], vrow[:, :], msk[0:NVEC, IDENT:IDENT + NVEC]).then_inc(vec_turned, 1)
            pe.wait_ge(vec_ready, 1)
            for s in range(L):
                pe.wait_ge(ld_wg[s], 16)
                pe.wait_ge(ld_wo[s], 16)
                pe.wait_ge(ld_w1[s], 16)
                pe.wait_ge(ld_w2[s], 16)
                pe.wait_ge(wv_ready[s], 1)
                pe.wait_ge(gspread_ready[s], 1)
            run(pe, iteration)


_INS = ["L0_attn_X", "L0_attn_ln1_w", "L0_attn_ln1_b", "L0_attn_ln2_w", "L0_attn_ln2_b", "L0_attn_WQ", "L0_attn_WK",
        "L0_attn_WV", "L0_attn_gn_w", "L0_attn_gn_b", "L0_attn_WG", "L0_attn_WO", "L0_attn_ffn_w1", "L0_attn_ffn_b1",
        "L0_attn_ffn_w2", "L0_attn_ffn_b2", "L0_ffn_w_gate", "L0_ffn_w_up", "L0_ffn_w_down"]


def kernel(**inputs):
    import concourse.bacc as bacc
    from concourse.bass_utils import run_bass_kernel_spmd

    nc = bacc.Bacc("TRN2", target_bir_lowering=False, num_devices=1)
    arrays, args = {}, []
    given = [(name, np.ascontiguousarray(inputs[name])) for name in _INS] + list(constants().items())
    for name, a in given:
        arrays[f"in_{name}"] = a
        args.append(nc.dram_tensor(f"in_{name}", a.shape, mybir.dt.from_np(a.dtype), kind="ExternalInput").ap())
    out = nc.dram_tensor("out", (B, S, D), F32, kind="ExternalOutput").ap()
    retention_kernel(nc, *args, out)
    r = run_bass_kernel_spmd(nc, [arrays], core_ids=[0])
    return r.results[0]["out"]
```

```python
from contextlib import ExitStack

import numpy as np

import concourse.bass as bass
from concourse import mybir

F32 = mybir.dt.float32
I32 = mybir.dt.int32
ALU = mybir.AluOpType
ACT = mybir.ActivationFunctionType
AX_X = mybir.AxisListType.X

P = 128
B, S, D = 8, 256, 128
L, H = 2, 8
HD = D // H
FFN = 512
HID = 384
T = S // P
G = 4
NF = FFN // P
NS = HID // P
EPS = 1e-5
QSCALE = float(np.float32(1.0 / 127.0))
SLOTS = 2
N = B * L // SLOTS
LOOP_START, LOOP_END = 2, N - 2
LN1W, LN1B, LN2W, LN2B, GNB, B1 = 0, L, 2 * L, 3 * L, 4 * L, 5 * L
NVEC = 5 * L + L * NF


def constants():
    half = HD // 2
    pos = np.arange(S, dtype=np.float64)
    scale = ((np.arange(0, HD, 2) + 0.4 * HD) / (1.4 * HD))[None, :] ** (pos / 64)[:, None]
    ang = pos[:, None] * (1.0 / 10000.0 ** (np.arange(half, dtype=np.float64) / half))[None, :]
    gamma = 1.0 - np.exp(np.linspace(np.log(1.0 / 32), np.log(1.0 / 64), H))
    sign = np.tile([-1.0, 1.0], half)
    cos, sin = np.empty((S, 2, H, HD)), np.empty((S, 2, H, HD))
    for part, (sc, g) in enumerate(((scale, 1.0), (1.0 / scale, -1.0))):
        decay = gamma[None, :] ** (g * pos[:, None])
        cos[:, part] = np.repeat(np.cos(ang) * sc, 2, -1)[:, None, :] * decay[:, :, None]
        sin[:, part] = (np.repeat(np.sin(ang) * sc, 2, -1) * sign)[:, None, :] * decay[:, :, None]
    tile = lambda a: a.reshape(T, P, 2 * D).transpose(1, 0, 2).reshape(P, T * 2 * D)
    f = np.arange(P)
    rotation = np.concatenate([tile(cos), tile(sin)], 1).astype(np.float32)
    masks = np.concatenate([
        np.eye(P),
        f[None, :] >= f[:, None],
        f[None, :] // HD == f[:, None] // HD,
        (np.arange(H)[None, :] == f[:, None] // HD) / HD,
        ((f // HD) % 2 == 0)[:, None], ((f // HD) % 2 == 1)[:, None],
    ], 1).astype(np.float32)
    spread = (np.arange(T * H)[:, None, None] == (np.arange(T)[:, None] * H + f[None, :] // HD)[None]).astype(np.float32)
    return {"rotation": rotation, "masks": masks, "spread": spread.reshape(T * H, T * D)}


IDENT, CAUSAL, SAMEHEAD, HEADMEAN, EVENODD = 0, P, 2 * P, 3 * P, 3 * P + H
NMASK = 3 * P + H + 2


def retention_kernel(nc, x, ln1_w, ln1_b, ln2_w, ln2_b, WQ, WK, WV, gn_w, gn_b, WG, WO,
                     ffn_w1, ffn_b1, ffn_w2, ffn_b2, w_gate, w_up, w_down,
                     rotation, masks, spread, out):
    ctx = ExitStack()
    with ctx:
        def sb(name, shape, dt=F32):
            return ctx.enter_context(nc.sbuf_tensor(name, shape, dt))

        def sem(name):
            return ctx.enter_context(nc.semaphore(name))

        def sem2(name):
            return [sem(f"{name}{k}") for k in range(2)]

        xall = sb("xall", [P, B * T, D])
        rot = sb("rot", [P, 2, T, 2 * D])
        msk = sb("msk", [P, NMASK])
        spr = sb("spr", [T * H, T, D])
        wqkv = [sb(f"wqkv{s}", [P, 3, H, HD]) for s in range(L)]
        wg = [sb(f"wg{s}", [P, D]) for s in range(L)]
        wo = [sb(f"wo{s}", [P, D]) for s in range(L)]
        w1 = [sb(f"w1_{s}", [P, FFN]) for s in range(L)]
        w2 = [sb(f"w2_{s}", [P, NF, D]) for s in range(L)]
        b2 = [sb(f"b2_{s}", [P, D]) for s in range(L)]
        gw = [sb(f"gw{s}", [T * H, D]) for s in range(L)]
        gspread = [sb(f"gspread{s}", [T * H, T, D]) for s in range(L)]
        vrow = sb("vrow", [NVEC, P])
        vcol = sb("vcol", [P, NVEC])
        vmean = [sb(f"vmean{s}", [P, H]) for s in range(L)]
        half = sb("half", [P, T * H])
        eps = sb("eps", [P, T])
        act_warm = sb("act_warm", [P, 1])
        qint = [sb(f"qint{k}", [P, NS, P], I32) for k in range(3)]
        qflt = [sb(f"qflt{k}", [P, NS, P]) for k in range(3)]
        sw = [sb(f"sw{k}", [P, NS, P]) for k in range(3)]
        xn = sb("xn", [P, T, D])
        lin = [sb(f"lin{s}", [P, B * T, D]) for s in range(L)]
        nst = SLOTS * 2 + 1
        st = [sb(f"st{k}", [P, T, 6]) for k in range(nst)]
        mv = [sb(f"mv{k}", [P, T, 2]) for k in range(nst)]
        ve = [sb(f"ve{k}", [P, T]) for k in range(nst)]
        rs = [sb(f"rs{k}", [P, T]) for k in range(nst)]
        nrm = [sb(f"nrm{s}", [P, T, D]) for s in range(L)]
        xT = [sb(f"xT{s}", [P, S]) for s in range(L)]
        rcos = [sb(f"rcos{s}", [P, T, 2 * D]) for s in range(L)]
        rsin = [sb(f"rsin{s}", [P, T, 2 * D]) for s in range(L)]
        qk = [sb(f"qk{s}", [P, T, 2 * D]) for s in range(L)]
        vpad = [sb(f"vpad{s}", [P, T, G, 4, HD]) for s in range(L)]
        gT = [sb(f"gT{s}", [P, S]) for s in range(L)]
        qT = [sb(f"qT{s}", [P, S]) for s in range(L)]
        kT = [sb(f"kT{s}", [P, 2, S]) for s in range(L)]
        stm = [sb(f"stm{s}", [P, D]) for s in range(L)]
        sc = [sb(f"sc{s}", [P, G, 2 * T, P]) for s in range(L)]
        scraw = [sb(f"scraw{s}", [P, 2 * T, P]) for s in range(L)]
        yT = [sb(f"yT{s}", [P, S]) for s in range(L)]
        ysq = [sb(f"ysq{s}", [P, S]) for s in range(L)]
        gve = [sb(f"gve{s}", [P, T * H]) for s in range(L)]
        grs = [sb(f"grs{s}", [P, T * H]) for s in range(L)]
        grT = [sb(f"grT{s}", [T * H, P]) for s in range(L)]
        ys = [sb(f"ys{s}", [P, S]) for s in range(L)]
        zT = [sb(f"zT{s}", [P, S]) for s in range(L)]
        yres = [sb(f"yres{s}", [P, T, D]) for s in range(L)]
        yb = [sb(f"yb{s}", [P, T, D]) for s in range(L)]
        ybx = sb("ybx", [P, T, D])
        nrm2 = [sb(f"nrm2_{s}", [P, T, D]) for s in range(L)]
        y2T = [sb(f"y2T{s}", [P, S]) for s in range(L)]
        hT = [sb(f"hT{s}", [P, NF, S]) for s in range(L)]
        snT = sb("snT", [P, S])
        sg = sb("sg", [P, NS, S])
        sh = sb("sh", [P, NS, S])

        SC = ctx.enter_context(nc.psum_tensor("SC", [P, G, 512], F32))
        A = [ctx.enter_context(nc.psum_tensor(f"A{s}", [P, 512], F32)) for s in range(L)]
        F = [ctx.enter_context(nc.psum_tensor(f"F{k}", [P, 512], F32)) for k in range(2)]

        ld_x0, ld_x, ld_msk, ld_vec, ld_rot, ld_spr, ld_q, ld_qdown = (sem(n) for n in ("ld_x0", "ld_x", "ld_msk", "ld_vec", "ld_rot", "ld_spr", "ld_q", "ld_qdown"))
        ld_qkv, ld_wg, ld_wo, ld_w1, ld_w2, ld_b2, ld_gw = (
            sem2(n) for n in ("ld_qkv", "ld_wg", "ld_wo", "ld_w1", "ld_w2", "ld_b2", "ld_gw"))
        vec_turned, vec_ready, half_ready, pad_ready, qflt_ready, sw_turned, sw_ready = (
            sem(n) for n in ("vec_turned", "vec_ready", "half_ready", "pad_ready", "qflt_ready", "sw_turned", "sw_ready"))
        wv_sum, wv_mean = sem("wv_sum"), sem("wv_mean")
        wv_ready, gspread_ready = sem2("wv_ready"), sem2("gspread_ready")
        ln_stats, ln_mv, ln_eps, ln_rstd, ln_done = (
            [sem(f"{n}{k}") for k in range(nst)] for n in ("ln_stats", "ln_mv", "ln_eps", "ln_rstd", "ln_done"))
        x_turned, xT_ready, qkv_done, g_done, rot_parts, qk_ready, v_ready, g_ready = (
            sem2(n) for n in ("x_turned", "xT_ready", "qkv_done", "g_done", "rot_parts", "qk_ready", "v_ready", "g_ready"))
        qk_turned, qkT_ready, state_done, scores_done, state_ready, y_done, yT_ready, ysq_ready = (
            sem2(n) for n in ("qk_turned", "qkT_ready", "state_done", "scores_done", "state_ready", "y_done", "yT_ready", "ysq_ready"))
        gvar_done, gvar_ready, grstd_ready, grstd_turned, grstdT_ready, grstd_spread, ys_ready, z_ready, o_done, yres_ready = (
            sem2(n) for n in ("gvar_done", "gvar_ready", "grstd_ready", "grstd_turned", "grstdT_ready", "grstd_spread",
                              "ys_ready", "z_ready", "o_done", "yres_ready"))
        masked = [[sem(f"masked{p}_{k}") for k in range(G - 1)] for p in range(SLOTS)]
        scores_copied, scores_pool = sem2("scores_copied"), sem2("scores_pool")
        yb_ready, y_turned, y2T_ready, ffn2_done, layer_ready = (
            sem2(n) for n in ("yb_ready", "y_turned", "y2T_ready", "ffn2_done", "layer_ready"))
        ffn1_done = [[sem(f"ffn1_done{s}_{k}") for k in range(2)] for s in range(L)]
        h_ready = [[sem(f"h_ready{s}_{k}") for k in range(2)] for s in range(L)]
        xn_kept, s_turned, snT_ready, down_done, side_ready, ybx_ready, stored = (
            sem(n) for n in ("xn_kept", "s_turned", "snT_ready", "down_done", "side_ready", "ybx_ready", "stored"))
        gu_done = [sem(f"gu_done{k}") for k in range(NS)]
        sg_ready = [sem(f"sg_ready{k}") for k in range(NS)]
        sh_ready = [sem(f"sh_ready{k}") for k in range(NS)]

        def on(n):
            return not isinstance(n, int) or 0 <= n < N

        def unit(p, n):
            if isinstance(n, int) and n == 0:
                return 0, p
            if isinstance(n, int) and n == N - 1:
                return 1, B - SLOTS + p
            return p, (n - 1 if p else n + 1)

        def in_layer(p, n, layer):
            return on(n) and unit(p, n)[0] == layer

        def wait(eng, s, value):
            if isinstance(value, int):
                if value > 0:
                    eng.wait_ge(s, value)
            else:
                eng.wait_ge(s, value)

        def passed(eng, s, n):
            wait(eng, s, n + 1)

        def bank_free(eng, *users):
            for s, n in users:
                if on(n):
                    passed(eng, s, n)
                    return

        def fresh(i):
            return isinstance(i, int) and i in (1, N - 1)

        def side_of(i):
            return unit(0, i)[1] if in_layer(0, i, 0) else -1

        def output_taken(p, n):
            if not on(n):
                return None, -1
            s, j = unit(p, n)
            return layer_ready[s], j

        def run(eng, iteration):
            for i in range(LOOP_START):
                iteration(i)
            with eng.Fori(LOOP_START, LOOP_END) as i:
                iteration(i)
            for i in range(LOOP_END, N + 1):
                iteration(i)

        col = lambda k: vcol[:, k:k + 1]
        ident = msk[:, IDENT:IDENT + P]

        vp_flat = [v[:, :, :, :, :].rearrange("p t g a k -> p t g (a k)") for v in vpad]

        def v_heads(p, t):
            v = vpad[p][:, t, :, :, :]
            return v[:, :, 0::3, :]

        SIDE_BANK = [1, 0, 0]
        FFN_BANK = [1, 0]
        MASK_ORDER = [(2, 3, 0), (0, 1, 2)]
        MASK_LAST = [1, 3]

        def tiles_of(buf, j):
            return buf[:, bass.ds(j * T, T), :]

        def tile_of(buf, j):
            return lambda t: buf[:, bass.ds(j * T + t, 1), :].rearrange("p a d -> p (a d)")

        block = ctx.enter_context(nc.Block())

        @block.sync
        def _(sp):
            x_v = x.rearrange("b (t p) d -> p (b t) d", p=P)
            sp.dma_start(xall[:, 0:T, :], x_v[:, 0:T, :]).then_inc(ld_x0, 16)
            sp.dma_start(msk[:, :], masks).then_inc(ld_msk, 16)
            for v, row in ((ln1_w, LN1W), (ln1_b, LN1B), (ln2_w, LN2W)):
                sp.dma_start(vrow[row:row + L, :], v).then_inc(ld_vec, 16)
            sp.dma_start(vrow[B1:B1 + L * NF, :], ffn_b1.rearrange("l (n p) -> (l n) p", p=P)).then_inc(ld_vec, 16)
            sp.dma_start(qint[2][:, :, :], w_down.rearrange("p (n q) -> p n q", n=NS)).then_inc(ld_qdown, 16)
            sp.dma_start(rot[:, :, :, :], rotation.rearrange("p (c t n) -> p c t n", c=2, t=T)).then_inc(ld_rot, 16)
            for s in range(L):
                sp.dma_start(gw[s][:, :], gn_w[s:s + 1, :].partition_broadcast(T * H)).then_inc(ld_gw[s], 16)
            for k, W in enumerate((WQ, WK, WV)):
                sp.dma_start(wqkv[1][:, k, :, :], W[1].rearrange("h d k -> d h k")).then_inc(ld_qkv[1], 16)

            o_v = out.rearrange("b (t p) d -> p (b t) d", p=P)

            def iteration(i):
                for p in range(SLOTS):
                    if not in_layer(p, i - 1, L - 1):
                        continue
                    j = unit(p, i - 1)[1]
                    passed(sp, layer_ready[L - 1], j)
                    sp.dma_start(o_v[:, bass.ds(j * T, T), :], tiles_of(xall, j)).then_inc(stored, 16)
            run(sp, iteration)
            sp.wait_ge(stored, 16 * B)

        @block.scalar
        def _(act):
            for k, W in enumerate((WQ, WK, WV)):
                act.dma_start(wqkv[0][:, k, :, :], W[0].rearrange("h d k -> d h k")).then_inc(ld_qkv[0], 16)
            for v, row in ((ln2_b, LN2B), (gn_b, GNB)):
                act.dma_start(vrow[row:row + L, :], v).then_inc(ld_vec, 16)
            act.dma_start(wg[0][:, :], WG[0]).then_inc(ld_wg[0], 16)
            act.dma_start(xall[:, T:, :], x.rearrange("b (t p) d -> p (b t) d", p=P)[:, T:, :]).then_inc(ld_x, 16)

            def x_affine(p, n):
                s, _ = unit(p, n)
                passed(act, x_turned[p], n)
                wait(act, g_done[p], n)
                nc.scalar.activation(xT[p][:, :], F[0][:, 0:S], ACT.Identity, bias=col(LN1B + s),
                                     scale=col(LN1W + s)).then_inc(xT_ready[p], 1)

            def keep_xn(j):
                passed(act, ln_done[0], j)
                nc.scalar.activation(tiles_of(lin[0], j), xn[:, :, :], ACT.Copy).then_inc(xn_kept, 1)

            def gate(p, n):
                passed(act, g_done[p], n)
                wait(act, z_ready[p], n)
                nc.scalar.activation(gT[p][:, :], A[p][:, 0:S], ACT.Silu).then_inc(g_ready[p], 1)

            def values(p, n):
                passed(act, rot_parts[p], n)
                wait(act, y_done[p], n)
                for t in range(T):
                    v = nc.scalar.activation(v_heads(p, t), SC[:, 2 * p + t, 2 * D:3 * D].rearrange(
                        "p (g a k) -> p g a k", g=G, a=2), ACT.Copy)
                v.then_inc(v_ready[p], 1)

            def qk_evacuate(p, n):
                passed(act, qk_turned[p], n)
                wait(act, y_done[p], n)
                nc.scalar.activation(qT[p][:, :], A[p][:, 0:S], ACT.Copy)
                for r in range(2):
                    k = nc.scalar.activation(kT[p][:, r, :], A[p][:, S:2 * S], ACT.Identity,
                                             scale=msk[:, EVENODD + r:EVENODD + r + 1])
                k.then_inc(qkT_ready[p], 1)

            def scores_copy(p, n):
                passed(act, scores_done[p], n)
                wait(act, scores_pool[p], n)
                nc.scalar.activation(scraw[p][:, :, :], SC[:, MASK_LAST[p], :].rearrange("p (a n) -> p a n", n=P),
                                     ACT.Copy).then_inc(scores_copied[p], 1)

            def y_evacuate(p, n):
                passed(act, y_done[p], n)
                wait(act, ys_ready[p], n)
                nc.scalar.activation(yT[p][:, :], A[p][:, 0:S], ACT.Copy).then_inc(yT_ready[p], 1)
                wait(act, gvar_done[p], n)
                nc.scalar.activation(ysq[p][:, :], A[p][:, 0:S], ACT.Square).then_inc(ysq_ready[p], 1)

            def y_affine(p, n):
                s, _ = unit(p, n)
                passed(act, y_turned[p], n)
                wait(act, ffn1_done[p][1], n)
                nc.scalar.activation(y2T[p][:, :], F[1][:, 0:S], ACT.Identity, bias=col(LN2B + s),
                                     scale=col(LN2W + s)).then_inc(y2T_ready[p], 1)

            def ffn_silu(p, k, n):
                s, _ = unit(p, n)
                wait(act, ffn2_done[p], n)
                passed(act, ffn1_done[p][k], n)
                for r in range(2):
                    f = 2 * k + r
                    h = nc.scalar.activation(hT[p][:, f, :], F[FFN_BANK[k]][:, r * S:(r + 1) * S], ACT.Silu,
                                             bias=col(B1 + s * NF + f))
                h.then_inc(h_ready[p][k], 1)

            def side_input(j):
                passed(act, s_turned, j)
                wait(act, gu_done[NS - 1], j)
                nc.scalar.activation(snT[:, :], F[1][:, 0:S], ACT.Copy).then_inc(snT_ready, 1)

            def side_silu(k, j):
                passed(act, gu_done[k], j)
                wait(act, sh_ready[k], j)
                nc.scalar.activation(sg[:, k, :], F[SIDE_BANK[k]][:, 0:S], ACT.Silu).then_inc(sg_ready[k], 1)

            def iteration(i):
                first = isinstance(i, int) and i == 0
                j = side_of(i)
                if first:
                    keep_xn(j)
                if on(j) and not first:
                    side_silu(0, j)
                if on(i):
                    gate(0, i)
                if first:
                    side_silu(0, j)
                if on(j) and not first:
                    keep_xn(j)
                if on(j):
                    side_silu(1, j)
                if on(i - 1):
                    y_evacuate(1, i - 1)
                if on(j) and not first:
                    side_silu(2, j)
                if on(i - 1):
                    y_affine(0, i - 1)
                if on(i):
                    values(0, i)
                    qk_evacuate(0, i)
                if on(i - 1):
                    ffn_silu(0, 0, i - 1)
                    ffn_silu(0, 1, i - 1)
                if on(i):
                    if fresh(i):
                        scores_copy(0, i)
                        x_affine(1, i)
                    else:
                        x_affine(1, i)
                        if first:
                            side_silu(2, j)
                        scores_copy(0, i)
                    gate(1, i)
                    y_evacuate(0, i)
                if on(i - 1):
                    y_affine(1, i - 1)
                if first:
                    keep_xn(1)
                    side_input(1)
                    side_silu(0, 1)
                    side_silu(1, 1)
                if on(i):
                    values(1, i)
                    qk_evacuate(1, i)
                if on(i - 1):
                    ffn_silu(1, 0, i - 1)
                    ffn_silu(1, 1, i - 1)
                if first:
                    side_silu(2, 1)
                if on(i + 1):
                    x_affine(0, i + 1)
                if on(side_of(i + 1)):
                    side_input(side_of(i + 1))
                if on(i):
                    scores_copy(1, i)

            act.wait_ge(half_ready, 1)
            nc.scalar.activation(act_warm[:, :], half[:, 0:1], ACT.Silu)
            act.wait_ge(vec_ready, 1)
            act.wait_ge(pad_ready, 1)
            x_affine(0, 0)
            side_input(0)
            run(act, iteration)

        @block.gpsimd
        def _(pool):
            nc.gpsimd.memset(half[:, :], -0.5)
            nc.gpsimd.memset(eps[:, :], EPS).then_inc(half_ready, 1)
            for p in range(SLOTS):
                last = nc.gpsimd.memset(vpad[p][:, :, :, :, :], 0.0)
            last.then_inc(pad_ready, 1)
            for k, W in enumerate((w_gate, w_up)):
                pool.dma_start(qint[k][:, :, :], W.rearrange("(n p) d -> p n d", p=P)).then_inc(ld_q, 16)
            pool.wait_ge(half_ready, 1)

            def ln_root(k, j):
                passed(pool, ln_mv[k], j)
                nc.gpsimd.tensor_tensor(ve[k][:, :], mv[k][:, :, 1], eps[:, :], ALU.add).then_inc(ln_eps[k], 1)
                passed(pool, ln_eps[k], j)
                wait(pool, ln_done[k], j)
                nc.gpsimd.tensor_tensor(rs[k][:, :], ve[k][:, :], half[:, 0:T], ALU.pow).then_inc(ln_rstd[k], 1)

            def rotate_sum(p, n):
                passed(pool, rot_parts[p], n)
                wait(pool, state_done[p], n)
                nc.gpsimd.tensor_tensor(qk[p][:, :, :], rcos[p][:, :, :], rsin[p][:, :, :], ALU.add).then_inc(qk_ready[p], 1)

            def group_root(p, n):
                passed(pool, gvar_ready[p], n)
                wait(pool, grstd_turned[p], n)
                nc.gpsimd.tensor_tensor(grs[p][:, :], gve[p][:, :], half[:, :], ALU.pow).then_inc(grstd_ready[p], 1)

            def residual_plus_bias(p, n):
                s, j = unit(p, n)
                passed(pool, yres_ready[p], n)
                nc.gpsimd.tensor_tensor(yb[p][:, :, :], yres[p][:, :, :],
                                        b2[s][:, :].unsqueeze(1).broadcast_to([P, T, D]), ALU.add).then_inc(yb_ready[p], 1)
                if s == L - 1:
                    passed(pool, yb_ready[p], n)
                    passed(pool, side_ready, j)
                    nc.gpsimd.tensor_tensor(ybx[:, :, :], yb[p][:, :, :], tiles_of(xall, j),
                                            ALU.add).then_inc(ybx_ready, 1)

            def later_loads():
                for s in range(L):
                    pool.dma_start(w1[s][:, :], ffn_w1[s]).then_inc(ld_w1[s], 16)
                    pool.dma_start(w2[s][:, :, :], ffn_w2[s].rearrange("(n p) d -> p n d", p=P)).then_inc(ld_w2[s], 16)
                    pool.dma_start(b2[s][:, :], ffn_b2[s:s + 1, :].partition_broadcast(P)).then_inc(ld_b2[s], 16)
                pool.dma_start(wg[1][:, :], WG[1]).then_inc(ld_wg[1], 16)
                pool.dma_start(wo[1][:, :], WO[1]).then_inc(ld_wo[1], 16)

            def mask_last(p, n):
                passed(pool, scores_copied[p], n)
                wait(pool, y_done[p], n)
                nc.gpsimd.tensor_tensor(sc[p][:, MASK_LAST[p], :, :], scraw[p][:, :, :],
                                        msk[:, CAUSAL:CAUSAL + P].unsqueeze(1).broadcast_to([P, 2 * T, P]),
                                        ALU.mult).then_inc(scores_pool[p], 1)

            def iteration(i):
                first = isinstance(i, int) and i == 0
                if first:
                    ln_root(0, 1)
                if on(i):
                    rotate_sum(0, i)
                if in_layer(1, i, 1) and not fresh(i):
                    ln_root(2, i)
                if first:
                    ln_root(2, 0)
                    later_loads()
                elif on(side_of(i + 1)):
                    ln_root(0, side_of(i + 1))
                if isinstance(i, int) and i == 1:
                    for s in range(L):
                        pool.wait_ge(ld_b2[s], 16)
                if on(i - 1):
                    group_root(1, i - 1)
                if not first and on(side_of(i + 1)):
                    ln_root(1, i + 1)
                if on(i - 1):
                    residual_plus_bias(0, i - 1)
                if in_layer(1, i, 1) and fresh(i):
                    ln_root(2, i)
                if on(i):
                    mask_last(0, i)
                if on(i - 1):
                    ln_root(4, i - 1)

                if on(i):
                    rotate_sum(1, i)
                    group_root(0, i)
                if first:
                    ln_root(0, 2)
                if first or in_layer(0, i + 1, 1):
                    ln_root(1, i + 1)
                if on(i - 1):
                    residual_plus_bias(1, i - 1)
                if on(i):
                    mask_last(1, i)
                    ln_root(3, i)

            ln_root(0, 0)
            ln_root(1, 0)
            pool.dma_start(wo[0][:, :], WO[0]).then_inc(ld_wo[0], 16)
            pool.dma_start(spr[:, :, :], spread.rearrange("p (t d) -> p t d", t=T)).then_inc(ld_spr, 16)
            run(pool, iteration)

        @block.vector
        def _(dve):
            def ln_statistics(k, src, n):
                wait(dve, ln_eps[k], n)
                if not isinstance(n, int):
                    passed(dve, ld_x, n)
                for t in range(T):
                    b = nc.vector.bn_stats(st[k][:, t, :], src(t))
                b.then_inc(ln_stats[k], 1)
                if not isinstance(n, int):
                    dve.wait_ge(ld_x, 16)
                passed(dve, ln_stats[k], n)
                for t in range(T):
                    b = nc.vector.bn_aggr(mv[k][:, t, :], st[k][:, t, :])
                b.then_inc(ln_mv[k], 1)

            def ln_normalise(k, dst, src, j):
                passed(dve, ln_rstd[k], j)
                for t in range(T):
                    b = nc.vector.tensor_scalar(dst[:, t, :], src(t), mv[k][:, t, 0:1], rs[k][:, t:t + 1],
                                                ALU.subtract, ALU.mult)
                b.then_inc(ln_done[k], 1)

            def tile(buf):
                return lambda t: buf[:, t, :]

            def input_stats(j):
                if isinstance(j, int) and j == 1:
                    dve.wait_ge(ld_x, 16)
                ln_statistics(0, tile_of(xall, j), j)

            def input_norm(j):
                if not (isinstance(j, int) and j == 0):
                    passed(dve, s_turned, j - 1)
                    passed(dve, xn_kept, j - 1)
                ln_normalise(0, xn, tile_of(xall, j), j)

            def layer_input(p, n):
                s, j = unit(p, n)
                return tile(xn) if s == 0 else tile_of(lin[1], j)

            def ln1_stats(p, n):
                s, j = unit(p, n)
                if s == 1:
                    dve.wait_ge(ld_x, 16)
                passed(dve, [ln_done[0], layer_ready[0]][s], j)
                ln_statistics(1 + p, layer_input(p, n), n)

            def ln1_norm(p, n):
                wait(dve, x_turned[p], n)
                ln_normalise(1 + p, nrm[p], layer_input(p, n), n)

            def rotate_cos(p, n):
                passed(dve, qkv_done[p], n)
                wait(dve, qk_ready[p], n)
                nc.vector.tensor_tensor(rcos[p][:, :, :], SC[:, 2 * p:2 * p + 2, 0:2 * D], rot[:, 0, :, :], ALU.mult)

            def rotate_sin(p, n):
                for t in range(T):
                    pairs = SC[:, 2 * p + t, 0:2 * D].rearrange("p (n a) -> p n a", a=2)[:, :, ::-1]
                    r = nc.vector.tensor_tensor(rsin[p][:, t, :].rearrange("p (n a) -> p n a", a=2), pairs,
                                                rot[:, 1, t, :].rearrange("p (n a) -> p n a", a=2), ALU.mult)
                r.then_inc(rot_parts[p], 1)

            def mask_state(p, n):
                passed(dve, state_done[p], n)
                wait(dve, y_done[p], n)
                nc.vector.tensor_tensor(stm[p][:, :], A[p][:, 0:D], msk[:, SAMEHEAD:SAMEHEAD + P],
                                        ALU.mult).then_inc(state_ready[p], 1)

            def mask_scores(p, k, n):
                if k == 0:
                    passed(dve, scores_done[p], n)
                    wait(dve, y_done[p], n)
                g = MASK_ORDER[p][k]
                nc.vector.tensor_tensor(sc[p][:, g, :, :], SC[:, g, :].rearrange("p (a n) -> p a n", n=P),
                                        msk[:, CAUSAL:CAUSAL + P].unsqueeze(1).broadcast_to([P, 2 * T, P]),
                                        ALU.mult).then_inc(masked[p][k], 1)

            def group_variance(p, n):
                passed(dve, gvar_done[p], n)
                wait(dve, grstd_ready[p], n)
                nc.vector.tensor_scalar(gve[p][:, :], A[p][:, 0:T * H], EPS, None, ALU.add).then_inc(gvar_ready[p], 1)

            def group_rstd(p, n):
                passed(dve, grstd_turned[p], n)
                wait(dve, grstd_spread[p], n)
                nc.vector.tensor_copy(grT[p][:, :], A[p][0:T * H, 0:P]).then_inc(grstdT_ready[p], 1)

            def gate_y(p, n):
                s, _ = unit(p, n)
                passed(dve, grstd_spread[p], n)
                passed(dve, yT_ready[p], n)
                nc.vector.tensor_tensor(ys[p][:, :], A[p][:, 0:S], yT[p][:, :], ALU.mult).then_inc(ys_ready[p], 1)
                passed(dve, ys_ready[p], n)
                passed(dve, g_ready[p], n)
                wait(dve, o_done[p], n)
                nc.vector.scalar_tensor_tensor(out=zT[p][:, :], in0=ys[p][:, :], scalar=col(GNB + s), in1=gT[p][:, :],
                                               op0=ALU.add, op1=ALU.mult).then_inc(z_ready[p], 1)

            def add_residual(p, n):
                s, j = unit(p, n)
                passed(dve, o_done[p], n)
                if s == 0:
                    passed(dve, xn_kept, j)
                wait(dve, yb_ready[p], n)
                nc.vector.tensor_tensor(yres[p][:, :, :], A[p][:, 0:S].rearrange("p (t d) -> p t d", t=T),
                                        tiles_of(lin[s], j), ALU.add).then_inc(yres_ready[p], 1)

            def ln2_stats(p, n):
                passed(dve, yres_ready[p], n)
                ln_statistics(3 + p, tile(yres[p]), n)

            def ln2_norm(p, n):
                wait(dve, y_turned[p], n)
                ln_normalise(3 + p, nrm2[p], tile(yres[p]), n)

            def layer_out(p, n):
                s, j = unit(p, n)
                passed(dve, ffn2_done[p], n)
                if s == 0:
                    passed(dve, yb_ready[p], n)
                else:
                    passed(dve, ybx_ready, j)
                nc.vector.tensor_tensor(tiles_of([lin[1], xall][s], j), F[1][:, 0:S].rearrange("p (t d) -> p t d", t=T),
                                        [yb[p], ybx][s][:, :, :], ALU.add).then_inc(layer_ready[s], 1)

            def side_product(k, j):
                passed(dve, sg_ready[k], j)
                wait(dve, down_done, j)
                nc.vector.tensor_tensor(sh[:, k, :], F[SIDE_BANK[k]][:, S:2 * S], sg[:, k, :], ALU.mult).then_inc(sh_ready[k], 1)

            def side_out(j):
                passed(dve, down_done, j)
                nc.vector.tensor_tensor(tiles_of(xall, j), F[0][:, 0:S].rearrange("p (t d) -> p t d", t=T),
                                        tiles_of(xall, j), ALU.add).then_inc(side_ready, 1)

            def side_weights():
                dve.wait_ge(ld_q, 32)
                dve.wait_ge(ld_qdown, 16)
                for k in range(3):
                    q = nc.vector.tensor_scalar(qflt[k][:, :, :], qint[k][:, :, :], QSCALE, None, ALU.mult)
                q.then_inc(qflt_ready, 1)

            def side_weights_out():
                dve.wait_ge(sw_turned, 1)
                for k in range(2):
                    nc.vector.tensor_copy(sw[k][:, :, :], SC[:, 2 + k, 0:NS * P].rearrange("p (n q) -> p n q", n=NS))
                nc.vector.tensor_copy(sw[2][:, :, :], A[1][:, 0:NS * P].rearrange("p (n q) -> p n q", n=NS)).then_inc(sw_ready, 1)

            def centre_values(s):
                dve.wait_ge(ld_qkv[s], 48)
                nc.vector.tensor_reduce(vmean[s][:, :], wqkv[s][:, 2, :, :], AX_X, ALU.add).then_inc(wv_sum, 1)
                dve.wait_ge(wv_sum, s + 1)
                nc.vector.tensor_scalar(vmean[s][:, :], vmean[s][:, :], -1.0 / HD, None, ALU.mult).then_inc(wv_mean, 1)
                dve.wait_ge(wv_mean, s + 1)
                nc.vector.tensor_tensor(wqkv[s][:, 2, :, :], wqkv[s][:, 2, :, :],
                                        vmean[s][:, :].unsqueeze(2).broadcast_to([P, H, HD]), ALU.add).then_inc(wv_ready[s], 1)

            def spread_weights(s):
                dve.wait_ge(ld_spr, 16)
                dve.wait_ge(ld_gw[s], 16)
                nc.vector.tensor_tensor(gspread[s][:, :, :], spr[:, :, :],
                                        gw[s][:, :].unsqueeze(1).broadcast_to([T * H, T, D]), ALU.mult).then_inc(gspread_ready[s], 1)

            def iteration(i):
                first = isinstance(i, int) and i == 0
                j, j_next = side_of(i), side_of(i + 1)
                if first:
                    rotate_cos(0, i)
                    rotate_sin(0, i)
                    input_norm(1)
                    ln1_stats(1, 0)
                    ln1_norm(1, 0)
                if on(j):
                    side_product(0, j)
                if on(i) and not first:
                    rotate_cos(0, i)
                    rotate_sin(0, i)
                if on(j):
                    side_product(1, j)
                if on(i - 1):
                    ln2_norm(0, i - 1)
                if in_layer(1, i, 1) and not fresh(i):
                    ln1_stats(1, i)
                if on(j_next) and not first:
                    input_stats(j_next)
                if on(i - 1):
                    group_variance(1, i - 1)
                if on(j):
                    side_product(2, j)
                if first:
                    spread_weights(0)
                if in_layer(1, i, 1) and not fresh(i):
                    ln1_norm(1, i)
                if on(j_next) and not first:
                    input_norm(j_next)
                    ln1_stats(0, i + 1)
                if on(i):
                    mask_state(0, i)
                if on(i - 1):
                    group_rstd(1, i - 1)
                if on(j_next) and not first:
                    ln1_norm(0, i + 1)
                if on(i - 1):
                    gate_y(1, i - 1)
                    layer_out(0, i - 1)
                if in_layer(1, i, 1) and fresh(i):
                    ln1_stats(1, i)
                if on(i):
                    mask_scores(0, 0, i)
                if in_layer(1, i, 1) and fresh(i):
                    ln1_norm(1, i)
                if on(i):
                    mask_scores(0, 1, i)
                if on(i - 1):
                    add_residual(1, i - 1)
                if on(i):
                    mask_scores(0, 2, i)
                if on(i - 1):
                    ln2_stats(1, i - 1)

                if on(i):
                    rotate_cos(1, i)
                    rotate_sin(1, i)
                if on(i - 1):
                    ln2_norm(1, i - 1)
                if on(i):
                    group_variance(0, i)
                if on(j):
                    side_out(j)
                if first:
                    centre_values(1)
                    spread_weights(1)
                    side_product(0, 1)
                    side_product(1, 1)
                    input_stats(2)
                    side_product(2, 1)
                    input_norm(2)
                if first or in_layer(0, i + 1, 1):
                    ln1_stats(0, i + 1)
                if on(i):
                    mask_state(1, i)
                    group_rstd(0, i)
                if first or in_layer(0, i + 1, 1):
                    ln1_norm(0, i + 1)
                if on(i - 1):
                    layer_out(1, i - 1)
                if on(i):
                    gate_y(0, i)
                if first:
                    side_out(1)
                if on(i):
                    mask_scores(1, 0, i)
                    mask_scores(1, 1, i)
                    add_residual(0, i)
                    mask_scores(1, 2, i)
                    ln2_stats(0, i)

            dve.wait_ge(ld_x0, 16)
            input_stats(0)
            input_norm(0)
            ln1_stats(0, 0)
            ln1_norm(0, 0)
            centre_values(0)
            dve.wait_ge(vec_turned, 1)
            nc.vector.tensor_copy(vcol[:, :], A[0][:, 0:NVEC]).then_inc(vec_ready, 1)
            side_weights()
            input_stats(1)
            side_weights_out()
            dve.wait_ge(ld_rot, 16)
            run(dve, iteration)

        @block.tensor
        def _(pe):
            mm = nc.tensor.matmul

            def x_turn(p, n):
                passed(pe, ln_done[1 + p], n)
                for t in range(T):
                    m = nc.tensor.transpose(F[0][:, t * P:(t + 1) * P], nrm[p][:, t, :], ident)
                m.then_inc(x_turned[p], 1)

            def project(p, n):
                s, _ = unit(p, n)
                passed(pe, xT_ready[p], n)
                for t in range(T):
                    bank_free(pe, (masked[1 - p][t], n if p else n - 1))
                    m = mm(SC[:, 2 * p + t, 0:3 * D], xT[p][:, t * P:(t + 1) * P],
                           wqkv[s][:, :, :, :].rearrange("p c h k -> p (c h k)"), start=True, stop=True)
                m.then_inc(qkv_done[p], 1)
                bank_free(pe, (yres_ready[p], n - 1))
                mm(A[p][:, 0:S], wg[s][:, :], xT[p][:, :], start=True, stop=True).then_inc(g_done[p], 1)

            def qk_turn(p, n):
                passed(pe, qk_ready[p], n)
                passed(pe, g_ready[p], n)
                for c in range(2):
                    for t in range(T):
                        m = nc.tensor.transpose(A[p][:, (c * T + t) * P:(c * T + t + 1) * P],
                                                qk[p][:, t, c * D:(c + 1) * D], ident)
                m.then_inc(qk_turned[p], 1)

            def state(p, n):
                passed(pe, qkT_ready[p], n)
                passed(pe, v_ready[p], n)
                mm(A[p][:, 0:D], qk[p][:, 0, D:2 * D], v_heads(p, 0), start=True, stop=True).then_inc(state_done[p], 1)

            def scores(p, r, t, n):
                if (r, t) == (0, 0):
                    passed(pe, qkT_ready[p], n)
                    passed(pe, v_ready[p], n)
                for g in range(G):
                    rows = slice(32 * g, 32 * g + 32)
                    m = mm(SC[:, g, (r * T + t) * P:(r * T + t + 1) * P], kT[p][rows, r, t * P:(t + 1) * P],
                           qT[p][rows, t * P:(t + 1) * P], start=True, stop=True)
                if (r, t) == (1, T - 1):
                    m.then_inc(scores_done[p], 1)

            def attend(p, n):
                for k in range(G - 1):
                    passed(pe, masked[p][k], n)
                passed(pe, scores_pool[p], n)
                passed(pe, state_ready[p], n)
                for r in range(2):
                    for t in range(T):
                        for g in range(G):
                            head = vp_flat[p][:, t, g, 32 * r:32 * r + 32]
                            mm(A[p][32 * g:32 * g + 32, t * P:(t + 1) * P], head, sc[p][:, g, r * T + t, :],
                               start=(r == 0 and t == 0), stop=(r == 1 and t == 0), skip_group_check=True)
                mm(A[p][:, P:2 * P], stm[p][:, :], qT[p][:, P:2 * P], start=False, stop=True,
                   skip_group_check=True).then_inc(y_done[p], 1)

            def variance(p, n):
                passed(pe, ysq_ready[p], n)
                for t in range(T):
                    m = mm(A[p][:, t * H:(t + 1) * H], ysq[p][:, t * P:(t + 1) * P], msk[:, HEADMEAN:HEADMEAN + H],
                           start=True, stop=True)
                m.then_inc(gvar_done[p], 1)

            def rstd_turn(p, n):
                passed(pe, grstd_ready[p], n)
                nc.tensor.transpose(A[p][0:T * H, 0:P], grs[p][:, :], ident).then_inc(grstd_turned[p], 1)

            def rstd_spread(p, n):
                s, _ = unit(p, n)
                passed(pe, grstdT_ready[p], n)
                for t in range(T):
                    m = mm(A[p][:, t * P:(t + 1) * P], gspread[s][:, t, :], grT[p][:, :], start=True, stop=True)
                m.then_inc(grstd_spread[p], 1)

            def project_out(p, n):
                s, _ = unit(p, n)
                passed(pe, z_ready[p], n)
                for t in range(T):
                    m = mm(A[p][:, t * P:(t + 1) * P], zT[p][:, t * P:(t + 1) * P], wo[s][:, :], start=True, stop=True)
                m.then_inc(o_done[p], 1)

            def y_turn(p, n):
                passed(pe, ln_done[3 + p], n)
                for t in range(T):
                    m = nc.tensor.transpose(F[1][:, t * P:(t + 1) * P], nrm2[p][:, t, :], ident)
                m.then_inc(y_turned[p], 1)

            def ffn_in(p, k, n):
                s, _ = unit(p, n)
                for r in range(2):
                    f = 2 * k + r
                    m = mm(F[FFN_BANK[k]][:, r * S:(r + 1) * S], w1[s][:, f * P:(f + 1) * P], y2T[p][:, :], start=True, stop=True)
                m.then_inc(ffn1_done[p][k], 1)

            def ffn_out(p, t, k, n):
                s, _ = unit(p, n)
                passed(pe, h_ready[p][k], n)
                for f in (2 * k, 2 * k + 1):
                    m = mm(F[1][:, t * P:(t + 1) * P], hT[p][:, f, t * P:(t + 1) * P], w2[s][:, f, :],
                           start=(f == 0), stop=(f == NF - 1))
                if (t, k) == (T - 1, 1):
                    m.then_inc(ffn2_done[p], 1)

            def side_turn(j):
                passed(pe, ln_done[0], j)
                for t in range(T):
                    m = nc.tensor.transpose(F[1][:, t * P:(t + 1) * P], xn[:, t, :], ident)
                m.then_inc(s_turned, 1)

            def side_in(k, j):
                passed(pe, snT_ready, j)
                b = F[SIDE_BANK[k]]
                mm(b[:, 0:S], sw[0][:, k, :], snT[:, :], start=True, stop=True)
                mm(b[:, S:2 * S], sw[1][:, k, :], snT[:, :], start=True, stop=True).then_inc(gu_done[k], 1)

            def side_down(t, j):
                for k in range(NS):
                    passed(pe, sh_ready[k], j)
                for k in range(NS):
                    m = mm(F[0][:, t * P:(t + 1) * P], sh[:, k, t * P:(t + 1) * P], sw[2][:, k, :],
                           start=(k == 0), stop=(k == NS - 1))
                if t == T - 1:
                    m.then_inc(down_done, 1)

            def side_weights():
                pe.wait_ge(qflt_ready, 1)
                for k in range(3):
                    b = [SC[:, 2, :], SC[:, 3, :], A[1][:, :]][k]
                    for n in range(NS):
                        m = nc.tensor.transpose(b[:, n * P:(n + 1) * P], qflt[k][:, n, :], ident)
                m.then_inc(sw_turned, 1)

            def iteration(i):
                first = isinstance(i, int) and i == 0
                j = side_of(i)
                if isinstance(i, int) and i == 1:
                    for s in range(L):
                        pe.wait_ge(ld_w1[s], 16)
                        pe.wait_ge(ld_w2[s], 16)
                    pe.wait_ge(ld_wo[1], 16)
                    pe.wait_ge(gspread_ready[1], 1)
                if on(i - 1):
                    project_out(0, i - 1)
                if on(j) and not first:
                    side_in(0, j)
                if on(i):
                    project(0, i)
                if first:
                    pe.wait_ge(sw_ready, 1)
                    side_in(0, j)
                if on(j):
                    side_in(1, j)
                if on(i - 1):
                    attend(1, i - 1)
                if on(j) and not first:
                    bank_free(pe, (sh_ready[1], j))
                    side_in(2, j)
                if on(i - 1):
                    bank_free(pe, (sh_ready[0], j), output_taken(1, i - 2))
                    y_turn(0, i - 1)
                if on(i):
                    qk_turn(0, i)
                if on(i - 1):
                    variance(1, i - 1)
                    passed(pe, y2T_ready[0], i - 1)
                    ffn_in(0, 0, i - 1)
                    bank_free(pe, (sh_ready[2], j), (xT_ready[0], i), (h_ready[1][1], i - 2))
                    ffn_in(0, 1, i - 1)
                if on(i):
                    bank_free(pe, (masked[1][2], i - 1))
                    bank_free(pe, (scores_copied[1], i - 1))
                    scores(0, 0, 0, i)
                    state(0, i)
                if on(i - 1):
                    ffn_out(0, 0, 0, i - 1)
                    ffn_out(0, 0, 1, i - 1)
                    rstd_turn(1, i - 1)
                if on(i):
                    scores(0, 0, 1, i)
                if on(i - 1):
                    rstd_spread(1, i - 1)
                    ffn_out(0, 1, 0, i - 1)
                if on(i) and not fresh(i):
                    bank_free(pe, (h_ready[0][1], i - 1), (sh_ready[1], j))
                    x_turn(1, i)
                if on(i):
                    scores(0, 1, 0, i)
                if first:
                    bank_free(pe, (xT_ready[1], i))
                    side_in(2, j)
                if on(i - 1):
                    ffn_out(0, 1, 1, i - 1)
                if on(i):
                    scores(0, 1, 1, i)
                if on(i - 1):
                    project_out(1, i - 1)
                if on(i) and fresh(i):
                    bank_free(pe, (h_ready[0][1], i - 1))
                    x_turn(1, i)
                if on(j):
                    bank_free(pe, (xT_ready[1], i))
                    side_down(0, j)
                if first:
                    pe.wait_ge(ld_wo[0], 16)
                    pe.wait_ge(gspread_ready[0], 1)
                if isinstance(i, int) and i == 1:
                    pe.wait_ge(ld_wg[1], 16)
                    pe.wait_ge(wv_ready[1], 1)
                if on(i):
                    project(1, i)
                    attend(0, i)
                if on(j):
                    side_down(1, j)
                if on(i - 1):
                    bank_free(pe, output_taken(0, i - 1))
                    y_turn(1, i - 1)
                if first:
                    side_turn(1)
                if on(i):
                    variance(0, i)
                if first:
                    side_in(0, 1)
                    bank_free(pe, (side_ready, j))
                    side_in(1, 1)
                if on(i):
                    qk_turn(1, i)
                if on(i - 1):
                    passed(pe, y2T_ready[1], i - 1)
                    ffn_in(1, 0, i - 1)
                if first:
                    bank_free(pe, (sh_ready[1], 1))
                    side_in(2, 1)
                if on(i - 1):
                    bank_free(pe, (side_ready, j), (h_ready[0][1], i - 1))
                    ffn_in(1, 1, i - 1)
                if on(i):
                    bank_free(pe, (masked[0][2], i))
                    bank_free(pe, (scores_copied[0], i))
                    scores(1, 0, 0, i)
                    state(1, i)
                if on(i - 1):
                    ffn_out(1, 0, 0, i - 1)
                    ffn_out(1, 0, 1, i - 1)
                if on(i):
                    rstd_turn(0, i)
                    scores(1, 0, 1, i)
                    rstd_spread(0, i)
                if on(i - 1):
                    ffn_out(1, 1, 0, i - 1)
                    ffn_out(1, 1, 1, i - 1)
                if on(i):
                    scores(1, 1, 0, i)
                if first:
                    for t in range(T):
                        side_down(t, 1)
                if on(i + 1):
                    bank_free(pe, (h_ready[1][1], i - 1), (side_ready, 1))
                    x_turn(0, i + 1)
                if on(side_of(i + 1)):
                    bank_free(pe, output_taken(1, i - 1), (sh_ready[0], 1))
                    side_turn(side_of(i + 1))
                if on(i):
                    scores(1, 1, 1, i)

            pe.wait_ge(ld_msk, 16)
            pe.wait_ge(ld_vec, 16 * 6)
            nc.tensor.transpose(A[0][:, 0:NVEC], vrow[:, :], msk[0:NVEC, IDENT:IDENT + NVEC]).then_inc(vec_turned, 1)
            pe.wait_ge(vec_ready, 1)
            x_turn(0, 0)
            side_turn(0)
            side_weights()
            pe.wait_ge(ld_wg[0], 16)
            pe.wait_ge(wv_ready[0], 1)
            run(pe, iteration)


_INS = ["L0_attn_X", "L0_attn_ln1_w", "L0_attn_ln1_b", "L0_attn_ln2_w", "L0_attn_ln2_b", "L0_attn_WQ", "L0_attn_WK",
        "L0_attn_WV", "L0_attn_gn_w", "L0_attn_gn_b", "L0_attn_WG", "L0_attn_WO", "L0_attn_ffn_w1", "L0_attn_ffn_b1",
        "L0_attn_ffn_w2", "L0_attn_ffn_b2", "L0_ffn_w_gate", "L0_ffn_w_up", "L0_ffn_w_down"]


def kernel(**inputs):
    import concourse.bacc as bacc
    from concourse.bass_utils import run_bass_kernel_spmd

    nc = bacc.Bacc("TRN2", target_bir_lowering=False, num_devices=1)
    arrays, args = {}, []
    given = [(name, np.ascontiguousarray(inputs[name])) for name in _INS] + list(constants().items())
    for name, a in given:
        arrays[f"in_{name}"] = a
        args.append(nc.dram_tensor(f"in_{name}", a.shape, mybir.dt.from_np(a.dtype), kind="ExternalInput").ap())
    out = nc.dram_tensor("out", (B, S, D), F32, kind="ExternalOutput").ap()
    retention_kernel(nc, *args, out)
    r = run_bass_kernel_spmd(nc, [arrays], core_ids=[0])
    return r.results[0]["out"]
```

```python
from contextlib import ExitStack

import numpy as np

import concourse.bass as bass
from concourse import mybir

F32 = mybir.dt.float32
I32 = mybir.dt.int32
ALU = mybir.AluOpType
ACT = mybir.ActivationFunctionType
AX_X = mybir.AxisListType.X

P = 128
B, S, D = 8, 256, 128
L, H = 2, 8
HD = D // H
FFN = 512
HID = 384
T = S // P
G = 4
NF = FFN // P
NS = HID // P
EPS = 1e-5
QSCALE = float(np.float32(1.0 / 127.0))
SLOTS = 2
N = B * L // SLOTS
LOOP_START, LOOP_END = 2, N - 2
LN1W, LN1B, LN2W, LN2B, GNB, B1 = 0, L, 2 * L, 3 * L, 4 * L, 5 * L
NVEC = 5 * L + L * NF


def constants():
    half = HD // 2
    pos = np.arange(S, dtype=np.float64)
    scale = ((np.arange(0, HD, 2) + 0.4 * HD) / (1.4 * HD))[None, :] ** (pos / 64)[:, None]
    ang = pos[:, None] * (1.0 / 10000.0 ** (np.arange(half, dtype=np.float64) / half))[None, :]
    gamma = 1.0 - np.exp(np.linspace(np.log(1.0 / 32), np.log(1.0 / 64), H))
    sign = np.tile([-1.0, 1.0], half)
    cos, sin = np.empty((S, 2, H, HD)), np.empty((S, 2, H, HD))
    for part, (sc, g) in enumerate(((scale, 1.0), (1.0 / scale, -1.0))):
        decay = gamma[None, :] ** (g * pos[:, None])
        cos[:, part] = np.repeat(np.cos(ang) * sc, 2, -1)[:, None, :] * decay[:, :, None]
        sin[:, part] = (np.repeat(np.sin(ang) * sc, 2, -1) * sign)[:, None, :] * decay[:, :, None]
    tile = lambda a: a.reshape(T, P, 2 * D).transpose(1, 0, 2).reshape(P, T * 2 * D)
    f = np.arange(P)
    rotation = np.concatenate([tile(cos), tile(sin)], 1).astype(np.float32)
    masks = np.concatenate([
        np.eye(P),
        f[None, :] >= f[:, None],
        f[None, :] // HD == f[:, None] // HD,
        (np.arange(H)[None, :] == f[:, None] // HD) / HD,
        ((f // HD) % 2 == 0)[:, None], ((f // HD) % 2 == 1)[:, None],
    ], 1).astype(np.float32)
    spread = np.arange(T * H)[:, None, None] == (np.arange(T)[:, None] * H + f[None, :] // HD)[None]
    return {"rotation": rotation, "masks": masks, "spread": spread.astype(np.float32).reshape(T * H, T * D)}


IDENT, CAUSAL, SAMEHEAD, HEADMEAN, EVENODD = 0, P, 2 * P, 3 * P, 3 * P + H
NMASK = 3 * P + H + 2


def retention_kernel(nc, x, ln1_w, ln1_b, ln2_w, ln2_b, WQ, WK, WV, gn_w, gn_b, WG, WO,
                     ffn_w1, ffn_b1, ffn_w2, ffn_b2, w_gate, w_up, w_down,
                     rotation, masks, spread, out):
    ctx = ExitStack()
    with ctx:
        def sb(name, shape, dt=F32):
            return ctx.enter_context(nc.sbuf_tensor(name, shape, dt))

        def sem(name):
            return ctx.enter_context(nc.semaphore(name))

        def sem2(name):
            return [sem(f"{name}{k}") for k in range(2)]

        xall = sb("xall", [P, B * T, D])
        rot = sb("rot", [P, 2, T, 2 * D])
        msk = sb("msk", [P, NMASK])
        spr = sb("spr", [T * H, T, D])
        wqkv = [sb(f"wqkv{s}", [P, 3, H, HD]) for s in range(L)]
        wg = [sb(f"wg{s}", [P, D]) for s in range(L)]
        wo = [sb(f"wo{s}", [P, D]) for s in range(L)]
        w1 = [sb(f"w1_{s}", [P, FFN]) for s in range(L)]
        w2 = [sb(f"w2_{s}", [P, NF, D]) for s in range(L)]
        b2 = [sb(f"b2_{s}", [P, D]) for s in range(L)]
        gw = [sb(f"gw{s}", [T * H, D]) for s in range(L)]
        gspread = [sb(f"gspread{s}", [T * H, T, D]) for s in range(L)]
        vrow = sb("vrow", [NVEC, P])
        vcol = sb("vcol", [P, NVEC])
        vmean = [sb(f"vmean{s}", [P, H]) for s in range(L)]
        half = sb("half", [P, T * H])
        eps = sb("eps", [P, T])
        act_warm = sb("act_warm", [P, 1])
        qint = [sb(f"qint{k}", [P, NS, P], I32) for k in range(3)]
        qflt = [sb(f"qflt{k}", [P, NS, P]) for k in range(3)]
        sw = [sb(f"sw{k}", [P, NS, P]) for k in range(3)]
        xn = sb("xn", [P, T, D])
        lin = [sb(f"lin{s}", [P, B * T, D]) for s in range(L)]
        nst = SLOTS * 2 + 1
        st = [sb(f"st{k}", [P, T, 6]) for k in range(nst)]
        mv = [sb(f"mv{k}", [P, T, 2]) for k in range(nst)]
        ve = [sb(f"ve{k}", [P, T]) for k in range(nst)]
        rs = [sb(f"rs{k}", [P, T]) for k in range(nst)]
        nrm = [sb(f"nrm{p}", [P, T, D]) for p in range(SLOTS)]
        xT = [sb(f"xT{p}", [P, S]) for p in range(SLOTS)]
        rcos = [sb(f"rcos{p}", [P, T, 2 * D]) for p in range(SLOTS)]
        rsin = [sb(f"rsin{p}", [P, T, 2 * D]) for p in range(SLOTS)]
        qk = [sb(f"qk{p}", [P, T, 2 * D]) for p in range(SLOTS)]
        vpad = [sb(f"vpad{p}", [P, T, G, 4, HD]) for p in range(SLOTS)]
        gT = [sb(f"gT{p}", [P, S]) for p in range(SLOTS)]
        qT = [sb(f"qT{p}", [P, S]) for p in range(SLOTS)]
        kT = [sb(f"kT{p}", [P, 2, S]) for p in range(SLOTS)]
        stm = [sb(f"stm{p}", [P, D]) for p in range(SLOTS)]
        sc = [sb(f"sc{p}", [P, G, 2 * T, P]) for p in range(SLOTS)]
        scraw = [sb(f"scraw{p}", [P, 2 * T, P]) for p in range(SLOTS)]
        yT = [sb(f"yT{p}", [P, S]) for p in range(SLOTS)]
        ysq = [sb(f"ysq{p}", [P, S]) for p in range(SLOTS)]
        gve = [sb(f"gve{p}", [P, T * H]) for p in range(SLOTS)]
        grs = [sb(f"grs{p}", [P, T * H]) for p in range(SLOTS)]
        grT = [sb(f"grT{p}", [T * H, P]) for p in range(SLOTS)]
        ys = [sb(f"ys{p}", [P, S]) for p in range(SLOTS)]
        zT = [sb(f"zT{p}", [P, S]) for p in range(SLOTS)]
        yres = [sb(f"yres{p}", [P, T, D]) for p in range(SLOTS)]
        yb = [sb(f"yb{p}", [P, T, D]) for p in range(SLOTS)]
        ybx = sb("ybx", [P, T, D])
        nrm2 = [sb(f"nrm2_{p}", [P, T, D]) for p in range(SLOTS)]
        y2T = [sb(f"y2T{p}", [P, S]) for p in range(SLOTS)]
        hT = [sb(f"hT{p}", [P, NF, S]) for p in range(SLOTS)]
        snT = sb("snT", [P, S])
        sg = sb("sg", [P, NS, S])
        sh = sb("sh", [P, NS, S])

        SC = ctx.enter_context(nc.psum_tensor("SC", [P, G, 512], F32))
        A = [ctx.enter_context(nc.psum_tensor(f"A{p}", [P, 512], F32)) for p in range(SLOTS)]
        F = [ctx.enter_context(nc.psum_tensor(f"F{k}", [P, 512], F32)) for k in range(2)]

        ld_x0, ld_x, ld_msk, ld_vec, ld_rot, ld_spr, ld_q, ld_qdown = (
            sem(n) for n in ("ld_x0", "ld_x", "ld_msk", "ld_vec", "ld_rot", "ld_spr", "ld_q", "ld_qdown"))
        ld_qkv, ld_wg, ld_wo, ld_w1, ld_w2, ld_b2, ld_gw = (
            sem2(n) for n in ("ld_qkv", "ld_wg", "ld_wo", "ld_w1", "ld_w2", "ld_b2", "ld_gw"))
        vec_turned, vec_ready, half_ready, pad_ready, qflt_ready, sw_turned, sw_ready = (
            sem(n) for n in ("vec_turned", "vec_ready", "half_ready", "pad_ready", "qflt_ready", "sw_turned", "sw_ready"))
        wv_sum, wv_mean = sem("wv_sum"), sem("wv_mean")
        wv_ready, gspread_ready = sem2("wv_ready"), sem2("gspread_ready")
        ln_stats, ln_mv, ln_eps, ln_rstd, ln_done = (
            [sem(f"{n}{k}") for k in range(nst)] for n in ("ln_stats", "ln_mv", "ln_eps", "ln_rstd", "ln_done"))
        x_turned, xT_ready, qkv_done, g_done, rot_parts, qk_ready, v_ready, g_ready = (
            sem2(n) for n in ("x_turned", "xT_ready", "qkv_done", "g_done", "rot_parts", "qk_ready", "v_ready", "g_ready"))
        qk_turned, qkT_ready, state_done, scores_done, state_ready, y_done, yT_ready, ysq_ready = (
            sem2(n) for n in ("qk_turned", "qkT_ready", "state_done", "scores_done", "state_ready", "y_done", "yT_ready", "ysq_ready"))
        gvar_done, gvar_ready, grstd_ready, grstd_turned, grstdT_ready, grstd_spread = (
            sem2(n) for n in ("gvar_done", "gvar_ready", "grstd_ready", "grstd_turned", "grstdT_ready", "grstd_spread"))
        ys_ready, z_ready, o_done, yres_ready = (sem2(n) for n in ("ys_ready", "z_ready", "o_done", "yres_ready"))
        masked = [[sem(f"masked{p}_{k}") for k in range(G - 1)] for p in range(SLOTS)]
        scores_copied, scores_pool = sem2("scores_copied"), sem2("scores_pool")
        yb_ready, y_turned, y2T_ready, ffn2_done, layer_ready = (
            sem2(n) for n in ("yb_ready", "y_turned", "y2T_ready", "ffn2_done", "layer_ready"))
        ffn1_done = [[sem(f"ffn1_done{p}_{k}") for k in range(2)] for p in range(SLOTS)]
        h_ready = [[sem(f"h_ready{p}_{k}") for k in range(2)] for p in range(SLOTS)]
        xn_kept, s_turned, snT_ready, down_done, side_ready, ybx_ready, stored = (
            sem(n) for n in ("xn_kept", "s_turned", "snT_ready", "down_done", "side_ready", "ybx_ready", "stored"))
        gu_done = [sem(f"gu_done{k}") for k in range(NS)]
        sg_ready = [sem(f"sg_ready{k}") for k in range(NS)]
        sh_ready = [sem(f"sh_ready{k}") for k in range(NS)]

        def on(n):
            return not isinstance(n, int) or 0 <= n < N

        def unit(p, n):
            if isinstance(n, int) and n == 0:
                return 0, p
            if isinstance(n, int) and n == N - 1:
                return 1, B - SLOTS + p
            return p, (n - 1 if p else n + 1)

        def in_layer(p, n, layer):
            return on(n) and unit(p, n)[0] == layer

        def wait(eng, s, value):
            if isinstance(value, int):
                if value > 0:
                    eng.wait_ge(s, value)
            else:
                eng.wait_ge(s, value)

        def passed(eng, s, n):
            wait(eng, s, n + 1)

        def bank_free(eng, *users):
            for s, n in users:
                if on(n):
                    passed(eng, s, n)
                    return

        def fresh(i):
            return isinstance(i, int) and i in (1, N - 1)

        def last_front(i):
            return isinstance(i, int) and i == N - 1

        def side_of(i):
            return unit(0, i)[1] if in_layer(0, i, 0) else -1

        def output_taken(p, n):
            if not on(n):
                return None, -1
            s, j = unit(p, n)
            return layer_ready[s], j

        def run(eng, iteration, ending):
            for i in range(LOOP_START):
                iteration(i)
            with eng.Fori(LOOP_START, LOOP_END) as i:
                iteration(i)
            for i in range(LOOP_END, N):
                iteration(i)
            ending()

        col = lambda k: vcol[:, k:k + 1]
        ident = msk[:, IDENT:IDENT + P]

        vp_flat = [v[:, :, :, :, :].rearrange("p t g a k -> p t g (a k)") for v in vpad]

        def v_heads(p, t):
            v = vpad[p][:, t, :, :, :]
            return v[:, :, 0::3, :]

        SIDE_BANK = [1, 0, 0]
        FFN_BANK = [1, 0]
        MASK_ORDER = [(2, 3, 0), (0, 1, 2)]
        MASK_LAST = [1, 3]

        def tiles_of(buf, j):
            return buf[:, bass.ds(j * T, T), :]

        def tile_of(buf, j):
            return lambda t: buf[:, bass.ds(j * T + t, 1), :].rearrange("p a d -> p (a d)")

        block = ctx.enter_context(nc.Block())

        @block.sync
        def _(sp):
            x_v = x.rearrange("b (t p) d -> p (b t) d", p=P)
            sp.dma_start(xall[:, 0:T, :], x_v[:, 0:T, :]).then_inc(ld_x0, 16)
            sp.dma_start(msk[:, :], masks).then_inc(ld_msk, 16)
            for v, row in ((ln1_w, LN1W), (ln1_b, LN1B), (ln2_w, LN2W)):
                sp.dma_start(vrow[row:row + L, :], v).then_inc(ld_vec, 16)
            sp.dma_start(vrow[B1:B1 + L * NF, :], ffn_b1.rearrange("l (n p) -> (l n) p", p=P)).then_inc(ld_vec, 16)
            sp.dma_start(qint[2][:, :, :], w_down.rearrange("p (n q) -> p n q", n=NS)).then_inc(ld_qdown, 16)
            sp.dma_start(rot[:, :, :, :], rotation.rearrange("p (c t n) -> p c t n", c=2, t=T)).then_inc(ld_rot, 16)
            for s in range(L):
                sp.dma_start(gw[s][:, :], gn_w[s:s + 1, :].partition_broadcast(T * H)).then_inc(ld_gw[s], 16)
            for k, W in enumerate((WQ, WK, WV)):
                sp.dma_start(wqkv[1][:, k, :, :], W[1].rearrange("h d k -> d h k")).then_inc(ld_qkv[1], 16)
            for s in range(L):
                sp.dma_start(w1[s][:, :], ffn_w1[s]).then_inc(ld_w1[s], 16)
                sp.dma_start(w2[s][:, :, :], ffn_w2[s].rearrange("(n p) d -> p n d", p=P)).then_inc(ld_w2[s], 16)
                sp.dma_start(b2[s][:, :], ffn_b2[s:s + 1, :].partition_broadcast(P)).then_inc(ld_b2[s], 16)
            sp.dma_start(wg[1][:, :], WG[1]).then_inc(ld_wg[1], 16)
            sp.dma_start(wo[1][:, :], WO[1]).then_inc(ld_wo[1], 16)

            o_v = out.rearrange("b (t p) d -> p (b t) d", p=P)

            def iteration(i):
                for p in range(SLOTS):
                    if not in_layer(p, i - 1, L - 1):
                        continue
                    j = unit(p, i - 1)[1]
                    passed(sp, layer_ready[L - 1], j)
                    sp.dma_start(o_v[:, bass.ds(j * T, T), :], tiles_of(xall, j)).then_inc(stored, 16)
            run(sp, iteration, lambda: iteration(N))
            sp.wait_ge(stored, 16 * B)

        @block.scalar
        def _(act):
            for k, W in enumerate((WQ, WK, WV)):
                act.dma_start(wqkv[0][:, k, :, :], W[0].rearrange("h d k -> d h k")).then_inc(ld_qkv[0], 16)
            for v, row in ((ln2_b, LN2B), (gn_b, GNB)):
                act.dma_start(vrow[row:row + L, :], v).then_inc(ld_vec, 16)
            act.dma_start(wg[0][:, :], WG[0]).then_inc(ld_wg[0], 16)
            act.dma_start(xall[:, T:, :], x.rearrange("b (t p) d -> p (b t) d", p=P)[:, T:, :]).then_inc(ld_x, 16)

            def x_affine(p, n):
                s, _ = unit(p, n)
                passed(act, x_turned[p], n)
                wait(act, g_done[p], n)
                nc.scalar.activation(xT[p][:, :], F[0][:, 0:S], ACT.Identity, bias=col(LN1B + s),
                                     scale=col(LN1W + s)).then_inc(xT_ready[p], 1)

            def keep_xn(j):
                passed(act, ln_done[0], j)
                nc.scalar.activation(tiles_of(lin[0], j), xn[:, :, :], ACT.Copy).then_inc(xn_kept, 1)

            def gate(p, n):
                passed(act, g_done[p], n)
                wait(act, z_ready[p], n)
                nc.scalar.activation(gT[p][:, :], A[p][:, 0:S], ACT.Silu).then_inc(g_ready[p], 1)

            def values(p, n):
                passed(act, rot_parts[p], n)
                wait(act, y_done[p], n)
                for t in range(T):
                    v = nc.scalar.activation(v_heads(p, t), SC[:, 2 * p + t, 2 * D:3 * D].rearrange(
                        "p (g a k) -> p g a k", g=G, a=2), ACT.Copy)
                v.then_inc(v_ready[p], 1)

            def qk_evacuate(p, n):
                passed(act, qk_turned[p], n)
                wait(act, y_done[p], n)
                nc.scalar.activation(qT[p][:, :], A[p][:, 0:S], ACT.Copy)
                for r in range(2):
                    k = nc.scalar.activation(kT[p][:, r, :], A[p][:, S:2 * S], ACT.Identity,
                                             scale=msk[:, EVENODD + r:EVENODD + r + 1])
                k.then_inc(qkT_ready[p], 1)

            def scores_copy(p, n):
                passed(act, scores_done[p], n)
                wait(act, scores_pool[p], n)
                nc.scalar.activation(scraw[p][:, :, :], SC[:, MASK_LAST[p], :].rearrange("p (a n) -> p a n", n=P),
                                     ACT.Copy).then_inc(scores_copied[p], 1)

            def y_evacuate(p, n):
                passed(act, y_done[p], n)
                wait(act, ys_ready[p], n)
                nc.scalar.activation(yT[p][:, :], A[p][:, 0:S], ACT.Copy).then_inc(yT_ready[p], 1)
                wait(act, gvar_done[p], n)
                nc.scalar.activation(ysq[p][:, :], A[p][:, 0:S], ACT.Square).then_inc(ysq_ready[p], 1)

            def y_affine(p, n):
                s, _ = unit(p, n)
                passed(act, y_turned[p], n)
                wait(act, ffn1_done[p][1], n)
                nc.scalar.activation(y2T[p][:, :], F[1][:, 0:S], ACT.Identity, bias=col(LN2B + s),
                                     scale=col(LN2W + s)).then_inc(y2T_ready[p], 1)

            def ffn_silu(p, k, n):
                s, _ = unit(p, n)
                wait(act, ffn2_done[p], n)
                passed(act, ffn1_done[p][k], n)
                for r in range(2):
                    f = 2 * k + r
                    h = nc.scalar.activation(hT[p][:, f, :], F[FFN_BANK[k]][:, r * S:(r + 1) * S], ACT.Silu,
                                             bias=col(B1 + s * NF + f))
                h.then_inc(h_ready[p][k], 1)

            def side_input(j):
                passed(act, s_turned, j)
                wait(act, gu_done[NS - 1], j)
                nc.scalar.activation(snT[:, :], F[1][:, 0:S], ACT.Copy).then_inc(snT_ready, 1)

            def side_silu(k, j):
                passed(act, gu_done[k], j)
                wait(act, sh_ready[k], j)
                nc.scalar.activation(sg[:, k, :], F[SIDE_BANK[k]][:, 0:S], ACT.Silu).then_inc(sg_ready[k], 1)

            def iteration(i):
                first = isinstance(i, int) and i == 0
                j = side_of(i)
                if first:
                    keep_xn(j)
                if on(j) and not first:
                    side_silu(0, j)
                if on(i):
                    gate(0, i)
                if first:
                    side_silu(0, j)
                if on(j) and not first:
                    keep_xn(j)
                if on(j):
                    side_silu(1, j)
                if on(i - 1):
                    y_evacuate(1, i - 1)
                if on(j) and not first:
                    side_silu(2, j)
                if on(i - 1):
                    y_affine(0, i - 1)
                if on(i):
                    values(0, i)
                    qk_evacuate(0, i)
                if on(i - 1):
                    ffn_silu(0, 0, i - 1)
                    ffn_silu(0, 1, i - 1)
                if on(i):
                    if fresh(i):
                        scores_copy(0, i)
                        x_affine(1, i)
                    else:
                        if first:
                            side_silu(2, j)
                        x_affine(1, i)
                        scores_copy(0, i)
                    gate(1, i)
                    y_evacuate(0, i)
                if on(i - 1) and not last_front(i):
                    y_affine(1, i - 1)
                if first:
                    keep_xn(1)
                    side_input(1)
                    side_silu(0, 1)
                    side_silu(1, 1)
                if on(i):
                    values(1, i)
                    if last_front(i):
                        y_affine(1, i - 1)
                    qk_evacuate(1, i)
                if on(i - 1):
                    ffn_silu(1, 0, i - 1)
                    ffn_silu(1, 1, i - 1)
                if first:
                    side_silu(2, 1)
                if on(i + 1):
                    x_affine(0, i + 1)
                if on(side_of(i + 1)):
                    side_input(side_of(i + 1))
                if on(i):
                    scores_copy(1, i)

            def ending():
                y_evacuate(1, N - 1)
                for p in range(SLOTS):
                    y_affine(p, N - 1)
                    for k in range(2):
                        ffn_silu(p, k, N - 1)

            act.wait_ge(half_ready, 1)
            nc.scalar.activation(act_warm[:, :], half[:, 0:1], ACT.Silu)
            act.wait_ge(vec_ready, 1)
            act.wait_ge(pad_ready, 1)
            x_affine(0, 0)
            side_input(0)
            run(act, iteration, ending)

        @block.gpsimd
        def _(pool):
            nc.gpsimd.memset(half[:, :], -0.5)
            nc.gpsimd.memset(eps[:, :], EPS).then_inc(half_ready, 1)
            for p in range(SLOTS):
                last = nc.gpsimd.memset(vpad[p][:, :, :, :, :], 0.0)
            last.then_inc(pad_ready, 1)
            for k, W in enumerate((w_gate, w_up)):
                pool.dma_start(qint[k][:, :, :], W.rearrange("(n p) d -> p n d", p=P)).then_inc(ld_q, 16)
            pool.wait_ge(half_ready, 1)

            def ln_root(k, j):
                passed(pool, ln_mv[k], j)
                nc.gpsimd.tensor_tensor(ve[k][:, :], mv[k][:, :, 1], eps[:, :], ALU.add).then_inc(ln_eps[k], 1)
                passed(pool, ln_eps[k], j)
                wait(pool, ln_done[k], j)
                nc.gpsimd.tensor_tensor(rs[k][:, :], ve[k][:, :], half[:, 0:T], ALU.pow).then_inc(ln_rstd[k], 1)

            def rotate_sum(p, n):
                passed(pool, rot_parts[p], n)
                wait(pool, state_done[p], n)
                nc.gpsimd.tensor_tensor(qk[p][:, :, :], rcos[p][:, :, :], rsin[p][:, :, :], ALU.add).then_inc(qk_ready[p], 1)

            def group_root(p, n):
                passed(pool, gvar_ready[p], n)
                wait(pool, grstd_turned[p], n)
                nc.gpsimd.tensor_tensor(grs[p][:, :], gve[p][:, :], half[:, :], ALU.pow).then_inc(grstd_ready[p], 1)

            def residual_plus_bias(p, n):
                s, j = unit(p, n)
                passed(pool, yres_ready[p], n)
                nc.gpsimd.tensor_tensor(yb[p][:, :, :], yres[p][:, :, :],
                                        b2[s][:, :].unsqueeze(1).broadcast_to([P, T, D]), ALU.add).then_inc(yb_ready[p], 1)
                if s == L - 1:
                    passed(pool, yb_ready[p], n)
                    passed(pool, side_ready, j)
                    nc.gpsimd.tensor_tensor(ybx[:, :, :], yb[p][:, :, :], tiles_of(xall, j),
                                            ALU.add).then_inc(ybx_ready, 1)

            def mask_last(p, n):
                passed(pool, scores_copied[p], n)
                wait(pool, y_done[p], n)
                nc.gpsimd.tensor_tensor(sc[p][:, MASK_LAST[p], :, :], scraw[p][:, :, :],
                                        msk[:, CAUSAL:CAUSAL + P].unsqueeze(1).broadcast_to([P, 2 * T, P]),
                                        ALU.mult).then_inc(scores_pool[p], 1)

            def iteration(i):
                first = isinstance(i, int) and i == 0
                if first:
                    ln_root(0, 1)
                if on(i):
                    rotate_sum(0, i)
                if in_layer(1, i, 1) and not fresh(i):
                    ln_root(2, i)
                if first:
                    ln_root(2, 0)
                if on(i - 1):
                    group_root(1, i - 1)
                if not first and on(side_of(i + 1)):
                    ln_root(0, side_of(i + 1))
                if isinstance(i, int) and i == 1:
                    for s in range(L):
                        pool.wait_ge(ld_b2[s], 16)
                if on(i - 1):
                    residual_plus_bias(0, i - 1)
                if in_layer(1, i, 1) and fresh(i):
                    ln_root(2, i)
                if on(i):
                    mask_last(0, i)
                if on(i - 1):
                    ln_root(4, i - 1)
                if on(i):
                    rotate_sum(1, i)
                    group_root(0, i)
                if first:
                    ln_root(0, 2)
                if on(i + 1):
                    ln_root(1, i + 1)
                if on(i - 1):
                    residual_plus_bias(1, i - 1)
                if on(i):
                    mask_last(1, i)
                    ln_root(3, i)

            def ending():
                group_root(1, N - 1)
                residual_plus_bias(0, N - 1)
                ln_root(4, N - 1)
                passed(pool, layer_ready[L - 1], unit(0, N - 1)[1])
                residual_plus_bias(1, N - 1)

            ln_root(0, 0)
            ln_root(1, 0)
            pool.dma_start(wo[0][:, :], WO[0]).then_inc(ld_wo[0], 16)
            pool.dma_start(spr[:, :, :], spread.rearrange("p (t d) -> p t d", t=T)).then_inc(ld_spr, 16)
            run(pool, iteration, ending)

        @block.vector
        def _(dve):
            def ln_statistics(k, src, n):
                wait(dve, ln_eps[k], n)
                if not isinstance(n, int):
                    passed(dve, ld_x, n)
                for t in range(T):
                    b = nc.vector.bn_stats(st[k][:, t, :], src(t))
                b.then_inc(ln_stats[k], 1)
                if not isinstance(n, int):
                    dve.wait_ge(ld_x, 16)
                passed(dve, ln_stats[k], n)
                for t in range(T):
                    b = nc.vector.bn_aggr(mv[k][:, t, :], st[k][:, t, :])
                b.then_inc(ln_mv[k], 1)

            def ln_normalise(k, dst, src, j):
                passed(dve, ln_rstd[k], j)
                for t in range(T):
                    b = nc.vector.tensor_scalar(dst[:, t, :], src(t), mv[k][:, t, 0:1], rs[k][:, t:t + 1],
                                                ALU.subtract, ALU.mult)
                b.then_inc(ln_done[k], 1)

            def tile(buf):
                return lambda t: buf[:, t, :]

            def input_stats(j):
                if isinstance(j, int) and j == 1:
                    dve.wait_ge(ld_x, 16)
                ln_statistics(0, tile_of(xall, j), j)

            def input_norm(j):
                if not (isinstance(j, int) and j == 0):
                    passed(dve, s_turned, j - 1)
                    passed(dve, xn_kept, j - 1)
                ln_normalise(0, xn, tile_of(xall, j), j)

            def layer_input(p, n):
                s, j = unit(p, n)
                return tile(xn) if s == 0 else tile_of(lin[1], j)

            def ln1_stats(p, n):
                s, j = unit(p, n)
                if s == 1:
                    dve.wait_ge(ld_x, 16)
                passed(dve, [ln_done[0], layer_ready[0]][s], j)
                ln_statistics(1 + p, layer_input(p, n), n)

            def ln1_norm(p, n):
                wait(dve, x_turned[p], n)
                ln_normalise(1 + p, nrm[p], layer_input(p, n), n)

            def rotate_cos(p, n):
                passed(dve, qkv_done[p], n)
                wait(dve, qk_ready[p], n)
                nc.vector.tensor_tensor(rcos[p][:, :, :], SC[:, 2 * p:2 * p + 2, 0:2 * D], rot[:, 0, :, :], ALU.mult)

            def rotate_sin(p, n):
                for t in range(T):
                    pairs = SC[:, 2 * p + t, 0:2 * D].rearrange("p (n a) -> p n a", a=2)[:, :, ::-1]
                    r = nc.vector.tensor_tensor(rsin[p][:, t, :].rearrange("p (n a) -> p n a", a=2), pairs,
                                                rot[:, 1, t, :].rearrange("p (n a) -> p n a", a=2), ALU.mult)
                r.then_inc(rot_parts[p], 1)

            def mask_state(p, n):
                passed(dve, state_done[p], n)
                wait(dve, y_done[p], n)
                nc.vector.tensor_tensor(stm[p][:, :], A[p][:, 0:D], msk[:, SAMEHEAD:SAMEHEAD + P],
                                        ALU.mult).then_inc(state_ready[p], 1)

            def mask_scores(p, k, n):
                if k == 0:
                    passed(dve, scores_done[p], n)
                    wait(dve, y_done[p], n)
                g = MASK_ORDER[p][k]
                nc.vector.tensor_tensor(sc[p][:, g, :, :], SC[:, g, :].rearrange("p (a n) -> p a n", n=P),
                                        msk[:, CAUSAL:CAUSAL + P].unsqueeze(1).broadcast_to([P, 2 * T, P]),
                                        ALU.mult).then_inc(masked[p][k], 1)

            def group_variance(p, n):
                passed(dve, gvar_done[p], n)
                wait(dve, grstd_ready[p], n)
                nc.vector.tensor_scalar(gve[p][:, :], A[p][:, 0:T * H], EPS, None, ALU.add).then_inc(gvar_ready[p], 1)

            def group_rstd(p, n):
                passed(dve, grstd_turned[p], n)
                wait(dve, grstd_spread[p], n)
                nc.vector.tensor_copy(grT[p][:, :], A[p][0:T * H, 0:P]).then_inc(grstdT_ready[p], 1)

            def gate_y(p, n):
                s, _ = unit(p, n)
                passed(dve, grstd_spread[p], n)
                passed(dve, yT_ready[p], n)
                nc.vector.tensor_tensor(ys[p][:, :], A[p][:, 0:S], yT[p][:, :], ALU.mult).then_inc(ys_ready[p], 1)
                passed(dve, ys_ready[p], n)
                passed(dve, g_ready[p], n)
                wait(dve, o_done[p], n)
                nc.vector.scalar_tensor_tensor(out=zT[p][:, :], in0=ys[p][:, :], scalar=col(GNB + s), in1=gT[p][:, :],
                                               op0=ALU.add, op1=ALU.mult).then_inc(z_ready[p], 1)

            def add_residual(p, n):
                s, j = unit(p, n)
                passed(dve, o_done[p], n)
                if s == 0:
                    passed(dve, xn_kept, j)
                wait(dve, yb_ready[p], n)
                nc.vector.tensor_tensor(yres[p][:, :, :], A[p][:, 0:S].rearrange("p (t d) -> p t d", t=T),
                                        tiles_of(lin[s], j), ALU.add).then_inc(yres_ready[p], 1)

            def ln2_stats(p, n):
                passed(dve, yres_ready[p], n)
                ln_statistics(3 + p, tile(yres[p]), n)

            def ln2_norm(p, n):
                wait(dve, y_turned[p], n)
                ln_normalise(3 + p, nrm2[p], tile(yres[p]), n)

            def layer_out(p, n):
                s, j = unit(p, n)
                passed(dve, ffn2_done[p], n)
                if s == 0:
                    passed(dve, yb_ready[p], n)
                else:
                    passed(dve, ybx_ready, j)
                nc.vector.tensor_tensor(tiles_of([lin[1], xall][s], j), F[1][:, 0:S].rearrange("p (t d) -> p t d", t=T),
                                        [yb[p], ybx][s][:, :, :], ALU.add).then_inc(layer_ready[s], 1)

            def side_product(k, j):
                passed(dve, sg_ready[k], j)
                wait(dve, down_done, j)
                nc.vector.tensor_tensor(sh[:, k, :], F[SIDE_BANK[k]][:, S:2 * S], sg[:, k, :],
                                        ALU.mult).then_inc(sh_ready[k], 1)

            def side_out(j):
                passed(dve, down_done, j)
                nc.vector.tensor_tensor(tiles_of(xall, j), F[0][:, 0:S].rearrange("p (t d) -> p t d", t=T),
                                        tiles_of(xall, j), ALU.add).then_inc(side_ready, 1)

            def side_weights():
                dve.wait_ge(ld_q, 32)
                dve.wait_ge(ld_qdown, 16)
                for k in range(3):
                    q = nc.vector.tensor_scalar(qflt[k][:, :, :], qint[k][:, :, :], QSCALE, None, ALU.mult)
                q.then_inc(qflt_ready, 1)

            def side_weights_out():
                dve.wait_ge(sw_turned, 1)
                for k in range(2):
                    nc.vector.tensor_copy(sw[k][:, :, :], SC[:, 2 + k, 0:NS * P].rearrange("p (n q) -> p n q", n=NS))
                nc.vector.tensor_copy(sw[2][:, :, :], A[1][:, 0:NS * P].rearrange(
                    "p (n q) -> p n q", n=NS)).then_inc(sw_ready, 1)

            def centre_values(s):
                dve.wait_ge(ld_qkv[s], 48)
                nc.vector.tensor_reduce(vmean[s][:, :], wqkv[s][:, 2, :, :], AX_X, ALU.add).then_inc(wv_sum, 1)
                dve.wait_ge(wv_sum, s + 1)
                nc.vector.tensor_scalar(vmean[s][:, :], vmean[s][:, :], -1.0 / HD, None, ALU.mult).then_inc(wv_mean, 1)
                dve.wait_ge(wv_mean, s + 1)
                nc.vector.tensor_tensor(wqkv[s][:, 2, :, :], wqkv[s][:, 2, :, :],
                                        vmean[s][:, :].unsqueeze(2).broadcast_to([P, H, HD]), ALU.add).then_inc(wv_ready[s], 1)

            def spread_weights(s):
                dve.wait_ge(ld_spr, 16)
                dve.wait_ge(ld_gw[s], 16)
                nc.vector.tensor_tensor(gspread[s][:, :, :], spr[:, :, :],
                                        gw[s][:, :].unsqueeze(1).broadcast_to([T * H, T, D]),
                                        ALU.mult).then_inc(gspread_ready[s], 1)

            def iteration(i):
                first = isinstance(i, int) and i == 0
                j, j_next = side_of(i), side_of(i + 1)
                if first:
                    rotate_cos(0, i)
                    rotate_sin(0, i)
                if on(j):
                    side_product(0, j)
                if first:
                    input_norm(1)
                if on(i) and not first:
                    rotate_cos(0, i)
                    rotate_sin(0, i)
                if on(j):
                    side_product(1, j)
                if first:
                    ln1_stats(1, 0)
                    ln1_norm(1, 0)
                if on(i - 1):
                    ln2_norm(0, i - 1)
                if in_layer(1, i, 1) and not fresh(i):
                    ln1_stats(1, i)
                if on(j_next) and not first:
                    input_stats(j_next)
                if on(i - 1):
                    group_variance(1, i - 1)
                if on(j):
                    side_product(2, j)
                if first:
                    spread_weights(0)
                if in_layer(1, i, 1) and not fresh(i):
                    ln1_norm(1, i)
                if on(i):
                    mask_state(0, i)
                if on(i - 1):
                    group_rstd(1, i - 1)
                if on(j_next) and not first:
                    input_norm(j_next)
                if on(i - 1):
                    if not fresh(i):
                        gate_y(1, i - 1)
                    layer_out(0, i - 1)
                if in_layer(1, i, 1) and fresh(i):
                    ln1_stats(1, i)
                    gate_y(1, i - 1)
                    ln1_norm(1, i)
                if on(i):
                    mask_scores(0, 0, i)
                    mask_scores(0, 1, i)
                if on(i - 1):
                    add_residual(1, i - 1)
                if on(i):
                    mask_scores(0, 2, i)
                if on(i - 1):
                    ln2_stats(1, i - 1)
                if on(i):
                    rotate_cos(1, i)
                    rotate_sin(1, i)
                if on(i - 1):
                    ln2_norm(1, i - 1)
                if on(i):
                    group_variance(0, i)
                if on(j):
                    side_out(j)
                if first:
                    centre_values(1)
                    spread_weights(1)
                    side_product(0, 1)
                    side_product(1, 1)
                    input_stats(2)
                    side_product(2, 1)
                    input_norm(2)
                if on(i + 1):
                    ln1_stats(0, i + 1)
                if on(i):
                    mask_state(1, i)
                    group_rstd(0, i)
                if on(i + 1):
                    ln1_norm(0, i + 1)
                if on(i - 1) and not last_front(i):
                    layer_out(1, i - 1)
                if on(i) and not last_front(i):
                    gate_y(0, i)
                if first:
                    side_out(1)
                if on(i):
                    mask_scores(1, 0, i)
                    mask_scores(1, 1, i)
                    if not last_front(i):
                        add_residual(0, i)
                    mask_scores(1, 2, i)
                if last_front(i):
                    gate_y(0, i)
                    add_residual(0, i)
                if on(i):
                    ln2_stats(0, i)
                if last_front(i):
                    layer_out(1, i - 1)

            def ending():
                group_variance(1, N - 1)
                ln2_norm(0, N - 1)
                group_rstd(1, N - 1)
                gate_y(1, N - 1)
                add_residual(1, N - 1)
                ln2_stats(1, N - 1)
                layer_out(0, N - 1)
                ln2_norm(1, N - 1)
                layer_out(1, N - 1)

            dve.wait_ge(ld_x0, 16)
            input_stats(0)
            input_norm(0)
            ln1_stats(0, 0)
            ln1_norm(0, 0)
            centre_values(0)
            dve.wait_ge(vec_turned, 1)
            nc.vector.tensor_copy(vcol[:, :], A[0][:, 0:NVEC]).then_inc(vec_ready, 1)
            side_weights()
            input_stats(1)
            side_weights_out()
            dve.wait_ge(ld_rot, 16)
            run(dve, iteration, ending)

        @block.tensor
        def _(pe):
            mm = nc.tensor.matmul

            def x_turn(p, n):
                passed(pe, ln_done[1 + p], n)
                for t in range(T):
                    m = nc.tensor.transpose(F[0][:, t * P:(t + 1) * P], nrm[p][:, t, :], ident)
                m.then_inc(x_turned[p], 1)

            def project(p, n):
                s, _ = unit(p, n)
                passed(pe, xT_ready[p], n)
                for t in range(T):
                    bank_free(pe, (masked[1 - p][t], n if p else n - 1))
                    m = mm(SC[:, 2 * p + t, 0:3 * D], xT[p][:, t * P:(t + 1) * P],
                           wqkv[s][:, :, :, :].rearrange("p c h k -> p (c h k)"), start=True, stop=True)
                m.then_inc(qkv_done[p], 1)
                bank_free(pe, (yres_ready[p], n - 1))
                mm(A[p][:, 0:S], wg[s][:, :], xT[p][:, :], start=True, stop=True).then_inc(g_done[p], 1)

            def qk_turn(p, n):
                passed(pe, qk_ready[p], n)
                passed(pe, g_ready[p], n)
                for c in range(2):
                    for t in range(T):
                        m = nc.tensor.transpose(A[p][:, (c * T + t) * P:(c * T + t + 1) * P],
                                                qk[p][:, t, c * D:(c + 1) * D], ident)
                m.then_inc(qk_turned[p], 1)

            def state(p, n):
                passed(pe, qkT_ready[p], n)
                passed(pe, v_ready[p], n)
                mm(A[p][:, 0:D], qk[p][:, 0, D:2 * D], v_heads(p, 0), start=True, stop=True).then_inc(state_done[p], 1)

            def scores(p, r, t, n):
                if (r, t) == (0, 0):
                    passed(pe, qkT_ready[p], n)
                    passed(pe, v_ready[p], n)
                for g in range(G):
                    rows = slice(32 * g, 32 * g + 32)
                    m = mm(SC[:, g, (r * T + t) * P:(r * T + t + 1) * P], kT[p][rows, r, t * P:(t + 1) * P],
                           qT[p][rows, t * P:(t + 1) * P], start=True, stop=True)
                if (r, t) == (1, T - 1):
                    m.then_inc(scores_done[p], 1)

            def attend(p, n):
                for k in range(G - 1):
                    passed(pe, masked[p][k], n)
                passed(pe, scores_pool[p], n)
                passed(pe, state_ready[p], n)
                for r in range(2):
                    for t in range(T):
                        for g in range(G):
                            head = vp_flat[p][:, t, g, 32 * r:32 * r + 32]
                            mm(A[p][32 * g:32 * g + 32, t * P:(t + 1) * P], head, sc[p][:, g, r * T + t, :],
                               start=(r == 0 and t == 0), stop=(r == 1 and t == 0), skip_group_check=True)
                mm(A[p][:, P:2 * P], stm[p][:, :], qT[p][:, P:2 * P], start=False, stop=True,
                   skip_group_check=True).then_inc(y_done[p], 1)

            def variance(p, n):
                passed(pe, ysq_ready[p], n)
                for t in range(T):
                    m = mm(A[p][:, t * H:(t + 1) * H], ysq[p][:, t * P:(t + 1) * P], msk[:, HEADMEAN:HEADMEAN + H],
                           start=True, stop=True)
                m.then_inc(gvar_done[p], 1)

            def rstd_turn(p, n):
                passed(pe, grstd_ready[p], n)
                nc.tensor.transpose(A[p][0:T * H, 0:P], grs[p][:, :], ident).then_inc(grstd_turned[p], 1)

            def rstd_spread(p, n):
                s, _ = unit(p, n)
                passed(pe, grstdT_ready[p], n)
                for t in range(T):
                    m = mm(A[p][:, t * P:(t + 1) * P], gspread[s][:, t, :], grT[p][:, :], start=True, stop=True)
                m.then_inc(grstd_spread[p], 1)

            def project_out(p, n):
                s, _ = unit(p, n)
                passed(pe, z_ready[p], n)
                for t in range(T):
                    m = mm(A[p][:, t * P:(t + 1) * P], zT[p][:, t * P:(t + 1) * P], wo[s][:, :], start=True, stop=True)
                m.then_inc(o_done[p], 1)

            def y_turn(p, n):
                passed(pe, ln_done[3 + p], n)
                for t in range(T):
                    m = nc.tensor.transpose(F[1][:, t * P:(t + 1) * P], nrm2[p][:, t, :], ident)
                m.then_inc(y_turned[p], 1)

            def ffn_in(p, k, n):
                s, _ = unit(p, n)
                for r in range(2):
                    f = 2 * k + r
                    m = mm(F[FFN_BANK[k]][:, r * S:(r + 1) * S], w1[s][:, f * P:(f + 1) * P], y2T[p][:, :],
                           start=True, stop=True)
                m.then_inc(ffn1_done[p][k], 1)

            def ffn_out(p, t, k, n):
                s, _ = unit(p, n)
                passed(pe, h_ready[p][k], n)
                for f in (2 * k, 2 * k + 1):
                    m = mm(F[1][:, t * P:(t + 1) * P], hT[p][:, f, t * P:(t + 1) * P], w2[s][:, f, :],
                           start=(f == 0), stop=(f == NF - 1))
                if (t, k) == (T - 1, 1):
                    m.then_inc(ffn2_done[p], 1)

            def side_turn(j):
                passed(pe, ln_done[0], j)
                for t in range(T):
                    m = nc.tensor.transpose(F[1][:, t * P:(t + 1) * P], xn[:, t, :], ident)
                m.then_inc(s_turned, 1)

            def side_in(k, j):
                passed(pe, snT_ready, j)
                b = F[SIDE_BANK[k]]
                mm(b[:, 0:S], sw[0][:, k, :], snT[:, :], start=True, stop=True)
                mm(b[:, S:2 * S], sw[1][:, k, :], snT[:, :], start=True, stop=True).then_inc(gu_done[k], 1)

            def side_down(t, j):
                for k in range(NS):
                    passed(pe, sh_ready[k], j)
                for k in range(NS):
                    m = mm(F[0][:, t * P:(t + 1) * P], sh[:, k, t * P:(t + 1) * P], sw[2][:, k, :],
                           start=(k == 0), stop=(k == NS - 1))
                if t == T - 1:
                    m.then_inc(down_done, 1)

            def side_weights():
                pe.wait_ge(qflt_ready, 1)
                for k in range(3):
                    b = [SC[:, 2, :], SC[:, 3, :], A[1][:, :]][k]
                    for n in range(NS):
                        m = nc.tensor.transpose(b[:, n * P:(n + 1) * P], qflt[k][:, n, :], ident)
                m.then_inc(sw_turned, 1)

            def iteration(i):
                first = isinstance(i, int) and i == 0
                j = side_of(i)
                if isinstance(i, int) and i == 1:
                    for s in range(L):
                        pe.wait_ge(ld_w1[s], 16)
                        pe.wait_ge(ld_w2[s], 16)
                    pe.wait_ge(ld_wo[1], 16)
                    pe.wait_ge(gspread_ready[1], 1)
                if on(i - 1):
                    project_out(0, i - 1)
                if on(j) and not first:
                    side_in(0, j)
                if on(i):
                    project(0, i)
                if first:
                    pe.wait_ge(sw_ready, 1)
                    side_in(0, j)
                if on(j):
                    side_in(1, j)
                if on(i - 1):
                    attend(1, i - 1)
                if on(j) and not first:
                    bank_free(pe, (sh_ready[1], j))
                    side_in(2, j)
                if on(i - 1):
                    bank_free(pe, (sh_ready[0], j), output_taken(1, i - 2))
                    y_turn(0, i - 1)
                if on(i):
                    qk_turn(0, i)
                if first:
                    bank_free(pe, (sh_ready[1], j))
                    side_in(2, j)
                if on(i - 1):
                    variance(1, i - 1)
                    passed(pe, y2T_ready[0], i - 1)
                    ffn_in(0, 0, i - 1)
                    bank_free(pe, (sh_ready[2], j), (xT_ready[0], i), (h_ready[1][1], i - 2))
                    ffn_in(0, 1, i - 1)
                if on(i):
                    bank_free(pe, (masked[1][2], i - 1))
                    bank_free(pe, (scores_copied[1], i - 1))
                    scores(0, 0, 0, i)
                    state(0, i)
                if on(i - 1):
                    ffn_out(0, 0, 0, i - 1)
                    ffn_out(0, 0, 1, i - 1)
                    rstd_turn(1, i - 1)
                    if fresh(i):
                        ffn_out(0, 1, 0, i - 1)
                        ffn_out(0, 1, 1, i - 1)
                if on(i):
                    scores(0, 0, 1, i)
                if on(i - 1):
                    rstd_spread(1, i - 1)
                    if not fresh(i):
                        ffn_out(0, 1, 0, i - 1)
                if on(i) and not fresh(i):
                    bank_free(pe, (h_ready[0][1], i - 1), (sh_ready[2], j))
                    x_turn(1, i)
                if on(i):
                    scores(0, 1, 0, i)
                if on(i - 1) and not fresh(i):
                    ffn_out(0, 1, 1, i - 1)
                if on(i):
                    scores(0, 1, 1, i)
                if on(i) and fresh(i):
                    bank_free(pe, (h_ready[0][1], i - 1))
                    x_turn(1, i)
                if on(i - 1):
                    project_out(1, i - 1)
                if on(j):
                    bank_free(pe, (xT_ready[1], i))
                    side_down(0, j)
                if first:
                    pe.wait_ge(ld_wo[0], 16)
                    pe.wait_ge(gspread_ready[0], 1)
                if isinstance(i, int) and i == 1:
                    pe.wait_ge(ld_wg[1], 16)
                    pe.wait_ge(wv_ready[1], 1)
                if on(i):
                    project(1, i)
                    attend(0, i)
                if on(j):
                    side_down(1, j)
                if on(i - 1):
                    bank_free(pe, output_taken(0, i - 1))
                    y_turn(1, i - 1)
                if last_front(i):
                    qk_turn(1, i)
                if first:
                    side_turn(1)
                if on(i):
                    variance(0, i)
                if first:
                    side_in(0, 1)
                    bank_free(pe, (side_ready, j))
                    side_in(1, 1)
                if on(i) and not last_front(i):
                    qk_turn(1, i)
                if on(i - 1):
                    passed(pe, y2T_ready[1], i - 1)
                    ffn_in(1, 0, i - 1)
                if first:
                    bank_free(pe, (sh_ready[1], 1))
                    side_in(2, 1)
                if on(i - 1):
                    bank_free(pe, (side_ready, j), (h_ready[0][1], i - 1))
                    ffn_in(1, 1, i - 1)
                if on(i):
                    bank_free(pe, (masked[0][2], i))
                    bank_free(pe, (scores_copied[0], i))
                    scores(1, 0, 0, i)
                    state(1, i)
                if last_front(i):
                    scores(1, 0, 1, i)
                    rstd_turn(0, i)
                    scores(1, 1, 0, i)
                    scores(1, 1, 1, i)
                    rstd_spread(0, i)
                if on(i - 1):
                    ffn_out(1, 0, 0, i - 1)
                    ffn_out(1, 0, 1, i - 1)
                if last_front(i):
                    attend(1, i)
                    project_out(0, i)
                if on(i) and not last_front(i):
                    rstd_turn(0, i)
                    scores(1, 0, 1, i)
                    rstd_spread(0, i)
                if on(i - 1):
                    ffn_out(1, 1, 0, i - 1)
                    ffn_out(1, 1, 1, i - 1)
                if on(i) and not last_front(i):
                    scores(1, 1, 0, i)
                if first:
                    for t in range(T):
                        side_down(t, 1)
                if on(i + 1):
                    bank_free(pe, (h_ready[1][1], i - 1), (side_ready, 1))
                    x_turn(0, i + 1)
                if on(side_of(i + 1)):
                    bank_free(pe, output_taken(1, i - 1), (sh_ready[0], 1))
                    side_turn(side_of(i + 1))
                if on(i) and not last_front(i):
                    scores(1, 1, 1, i)

            def ending():
                n = N - 1
                variance(1, n)
                bank_free(pe, output_taken(1, n - 1))
                y_turn(0, n)
                passed(pe, y2T_ready[0], n)
                ffn_in(0, 0, n)
                rstd_turn(1, n)
                bank_free(pe, (h_ready[1][1], n - 1))
                ffn_in(0, 1, n)
                rstd_spread(1, n)
                ffn_out(0, 0, 0, n)
                ffn_out(0, 0, 1, n)
                project_out(1, n)
                ffn_out(0, 1, 0, n)
                ffn_out(0, 1, 1, n)
                bank_free(pe, output_taken(0, n))
                y_turn(1, n)
                passed(pe, y2T_ready[1], n)
                ffn_in(1, 0, n)
                bank_free(pe, (h_ready[0][1], n))
                ffn_in(1, 1, n)
                for t in range(T):
                    for k in range(2):
                        ffn_out(1, t, k, n)

            pe.wait_ge(ld_msk, 16)
            pe.wait_ge(ld_vec, 16 * 6)
            nc.tensor.transpose(A[0][:, 0:NVEC], vrow[:, :], msk[0:NVEC, IDENT:IDENT + NVEC]).then_inc(vec_turned, 1)
            pe.wait_ge(vec_ready, 1)
            x_turn(0, 0)
            side_turn(0)
            side_weights()
            pe.wait_ge(ld_wg[0], 16)
            pe.wait_ge(wv_ready[0], 1)
            run(pe, iteration, ending)


_INS = ["L0_attn_X", "L0_attn_ln1_w", "L0_attn_ln1_b", "L0_attn_ln2_w", "L0_attn_ln2_b", "L0_attn_WQ", "L0_attn_WK",
        "L0_attn_WV", "L0_attn_gn_w", "L0_attn_gn_b", "L0_attn_WG", "L0_attn_WO", "L0_attn_ffn_w1", "L0_attn_ffn_b1",
        "L0_attn_ffn_w2", "L0_attn_ffn_b2", "L0_ffn_w_gate", "L0_ffn_w_up", "L0_ffn_w_down"]


def kernel(**inputs):
    import concourse.bacc as bacc
    from concourse.bass_utils import run_bass_kernel_spmd

    nc = bacc.Bacc("TRN2", target_bir_lowering=False, num_devices=1)
    arrays, args = {}, []
    given = [(name, np.ascontiguousarray(inputs[name])) for name in _INS] + list(constants().items())
    for name, a in given:
        arrays[f"in_{name}"] = a
        args.append(nc.dram_tensor(f"in_{name}", a.shape, mybir.dt.from_np(a.dtype), kind="ExternalInput").ap())
    out = nc.dram_tensor("out", (B, S, D), F32, kind="ExternalOutput").ap()
    retention_kernel(nc, *args, out)
    r = run_bass_kernel_spmd(nc, [arrays], core_ids=[0])
    return r.results[0]["out"]
```
